# Optimizing a Trainium2 kernel written in Bass

```python
import numpy as np
import jax
import jax.numpy as jnp

def _softmax(x, axis=-1):
    return jax.nn.softmax(x, axis=axis)

def _gelu(x):
    return jax.nn.gelu(x, approximate=True)

def _silu(x):
    return jax.nn.silu(x)

def _sigmoid(x):
    return jax.nn.sigmoid(x)

def _layernorm(x, axis=-1, eps=1e-05):
    m = jnp.mean(x, axis=axis, keepdims=True)
    v = jnp.var(x, axis=axis, keepdims=True)
    return (x - m) / jnp.sqrt(v + eps)

def _scatter_add(tgt, idx, src, axis=0):
    return tgt.at[idx].add(src)

def _segment_sum(src, seg, n):
    return jax.ops.segment_sum(src, seg, n)
kernel_name = 'mk_xattn_ffn_d2_seqx_r8_625b05'

def setup_inputs(seed: int=0):
    np.random.seed(seed)
    _w = jnp.asarray

    def _rec_inputs():
        import jax
        import jax.numpy as jnp
        _rk = jax.random.key(seed)
        x = -0.0003929 + 0.9999 * jax.random.normal(jax.random.fold_in(_rk, 1), (32, 64, 256), jnp.float32)
        _lenS = 64 - jax.random.randint(jax.random.fold_in(_rk, 7), (32,), 0, max(1, 64 // 4) + 1, jnp.int32)
        _lenS2 = 64 - jax.random.randint(jax.random.fold_in(_rk, 8), (32,), 0, max(1, 64 // 4) + 1, jnp.int32)
        _ctx_2048P = jax.random.normal(jax.random.fold_in(_rk, 11), (32, 16, 256), jnp.float32)
        _ctx_2048c = jax.random.dirichlet(jax.random.fold_in(_rk, 511), 0.3 * jnp.ones((16,), jnp.float32), (32, 64))
        _ctx_2048t = jnp.einsum('bsk,bkd->bsd', _ctx_2048c, _ctx_2048P)
        _ctx_2048t = _ctx_2048t * jax.lax.rsqrt(jnp.mean(jnp.square(_ctx_2048t)) + 1e-12) * 0.953939
        ctx_2048 = 2.81802e-05 + 1.00001 * (_ctx_2048t + 0.3 * jax.random.normal(jax.random.fold_in(_rk, 611), (32, 64, 256), jnp.float32))
        _validS = jnp.arange(64)[None, :] < _lenS[:, None]
        _validS2 = jnp.arange(64)[None, :] < _lenS2[:, None]
        _causal = jnp.tril(jnp.ones((64, 64), dtype=bool))
        mask_BxS2_bk0 = jnp.logical_not(jnp.broadcast_to(_validS2[:, :], (32, 64)))
        return (x, ctx_2048, mask_BxS2_bk0)
    x, ctx_2048, mask_BxS2_bk0 = _rec_inputs()

    def _L0_xattn_setup():
        import jax, jax.numpy as jnp
        import numpy as np
        NUM_HEADS = 8

        def _proj(W, x):
            return jnp.einsum('oi,bin->bon', W, x)

        def _split_heads(x, h):
            B, D, N = x.shape
            return x.reshape(B, D, h, N // h).transpose(2, 0, 1, 3)

        def _mha(XQ, XK, XV, Wq, Wk, Wv, Wo):
            B, D, N = XQ.shape
            h = NUM_HEADS
            Nh = N // h
            q = _split_heads(_proj(Wq, XQ), h)
            k = _split_heads(_proj(Wk, XK), h)
            v = _split_heads(_proj(Wv, XV), h)
            scores = jnp.einsum('hbdn,hben->hbde', q, k) / jnp.sqrt(jnp.asarray(Nh, q.dtype))
            p = jax.nn.softmax(scores, axis=-1)
            out = jnp.einsum('hbde,hben->hbdn', p, v)
            attn_heads = out.transpose(1, 2, 0, 3).reshape(B, D, N)
            return _proj(Wo, XQ - attn_heads)
        key = jax.random.key(seed)
        ks = jax.random.split(key, 7)
        B, D, N = (16, 64, 256)
        sc = 1.0 / np.sqrt(D)
        return {'X_Query': jax.random.normal(ks[0], (B, D, N), jnp.float32), 'X_Key': jax.random.normal(ks[1], (B, D, N), jnp.float32), 'X_Value': jax.random.normal(ks[2], (B, D, N), jnp.float32), 'W_q': jax.random.normal(ks[3], (D, D), jnp.float32) * sc, 'W_k': jax.random.normal(ks[4], (D, D), jnp.float32) * sc, 'W_v': jax.random.normal(ks[5], (D, D), jnp.float32) * sc, 'W_o': jax.random.normal(ks[6], (D, D), jnp.float32) * sc}
    _L0_xattn_all = _L0_xattn_setup()
    _L0_xattn_in = {k: v for k, v in _L0_xattn_all.items() if k in ('W_q', 'W_k', 'W_v', 'W_o')}
    del _L0_xattn_all

    def _L0_ffn_setup():
        import jax, jax.numpy as jnp
        import numpy as np
        E, K, D, INTER, SH_INTER = (16, 2, 256, 176, 352)
        ROUTE_SCALE = 1.0

        def _moe_forward(x, gate_w, w1, b1, w2, b2, w3, b3, sw1, sb1, sw2, sb2, sw3, sb3):
            shape = x.shape
            xt = x.reshape(-1, shape[-1])
            T = xt.shape[0]
            probs = jax.nn.softmax((xt @ gate_w.T).astype(jnp.float32), axis=-1)
            topw, topi = jax.lax.top_k(probs, K)
            weights = (topw * ROUTE_SCALE).astype(x.dtype)
            cw = jnp.zeros((T, E), x.dtype).at[jnp.arange(T)[:, None], topi].add(weights)

            def step(acc, p):
                W1, B1, W2, B2, W3, B3, wcol = p
                h = jax.nn.silu(xt @ W1.T + B1) * (xt @ W3.T + B3)
                return (acc + wcol[:, None] * (h @ W2.T + B2), None)
            y, _ = jax.lax.scan(step, jnp.zeros_like(xt), (w1, b1, w2, b2, w3, b3, cw.T))
            z = jax.nn.silu(xt @ sw1.T + sb1) * (xt @ sw3.T + sb3) @ sw2.T + sb2
            return (y + z).reshape(shape)
        key = jax.random.key(seed)
        k = jax.random.split(key, 14)
        s = jnp.float32(0.02)
        return {'x': jax.random.normal(k[0], (2, 64, D), jnp.float32), 'gate_w': jax.random.normal(k[1], (E, D), jnp.float32) * s, 'w1': jax.random.normal(k[2], (E, INTER, D), jnp.float32) * s, 'b1': jax.random.normal(k[3], (E, INTER), jnp.float32) * s, 'w2': jax.random.normal(k[4], (E, D, INTER), jnp.float32) * s, 'b2': jax.random.normal(k[5], (E, D), jnp.float32) * s, 'w3': jax.random.normal(k[6], (E, INTER, D), jnp.float32) * s, 'b3': jax.random.normal(k[7], (E, INTER), jnp.float32) * s, 'sw1': jax.random.normal(k[8], (SH_INTER, D), jnp.float32) * s, 'sb1': jax.random.normal(k[9], (SH_INTER,), jnp.float32) * s, 'sw2': jax.random.normal(k[10], (D, SH_INTER), jnp.float32) * s, 'sb2': jax.random.normal(k[11], (D,), jnp.float32) * s, 'sw3': jax.random.normal(k[12], (SH_INTER, D), jnp.float32) * s, 'sb3': jax.random.normal(k[13], (SH_INTER,), jnp.float32) * s}
    _L0_ffn_all = _L0_ffn_setup()
    _L0_ffn_in = {k: v for k, v in _L0_ffn_all.items() if k in ('gate_w', 'w1', 'b1', 'w2', 'b2', 'w3', 'b3', 'sw1', 'sb1', 'sw2', 'sb2', 'sw3', 'sb3')}
    del _L0_ffn_all

    def _L1_xattn_setup():
        import jax, jax.numpy as jnp
        import numpy as np
        key = jax.random.key(seed)
        k1, k2, k3 = jax.random.split(key, 3)
        B, S, D, M = (8, 256, 256, 128)
        hidden_states = jax.random.normal(k1, (B, S, D), dtype=jnp.float32)
        memory_tokens = jax.random.normal(k2, (B, M, D), dtype=jnp.float32)
        memory_mask = jax.random.randint(k3, (B, M), 0, 2).astype(jnp.bool_)
        return {'hidden_states': hidden_states, 'memory_tokens': memory_tokens, 'memory_mask': memory_mask}
    _L1_xattn_all = _L1_xattn_setup()
    _L1_xattn_in = {k: v for k, v in _L1_xattn_all.items() if k in ()}
    del _L1_xattn_all

    def _L1_ffn_setup():
        import jax, jax.numpy as jnp
        import numpy as np
        HID = 256
        N_EXP = 32
        F_EXP = 96
        TOP_K = 6
        F_SH = 192
        B, S = (1, 128)
        key = jax.random.key(seed)
        ks = jax.random.split(key, 8)
        s = 0.02
        return {'hidden_states': jax.random.normal(ks[0], (B, S, HID), dtype=jnp.float32), 'gate_w': jax.random.normal(ks[1], (HID, N_EXP), dtype=jnp.float32) * s, 'wg': jax.random.normal(ks[2], (N_EXP, HID, F_EXP), dtype=jnp.float32) * s, 'wu': jax.random.normal(ks[3], (N_EXP, HID, F_EXP), dtype=jnp.float32) * s, 'wd': jax.random.normal(ks[4], (N_EXP, F_EXP, HID), dtype=jnp.float32) * s, 'sg': jax.random.normal(ks[5], (HID, F_SH), dtype=jnp.float32) * s, 'su': jax.random.normal(ks[6], (HID, F_SH), dtype=jnp.float32) * s, 'sd': jax.random.normal(ks[7], (F_SH, HID), dtype=jnp.float32) * s}
    _L1_ffn_all = _L1_ffn_setup()
    _L1_ffn_in = {k: v for k, v in _L1_ffn_all.items() if k in ('gate_w', 'wg', 'wu', 'wd', 'sg', 'su', 'sd')}
    del _L1_ffn_all
    return {'x': x, 'ctx_2048': ctx_2048, 'mask_BxS2_bk0': mask_BxS2_bk0, 'L0_xattn_W_q': _L0_xattn_in['W_q'], 'L0_xattn_W_k': _L0_xattn_in['W_k'], 'L0_xattn_W_v': _L0_xattn_in['W_v'], 'L0_xattn_W_o': _L0_xattn_in['W_o'], 'L0_ffn_gate_w': _L0_ffn_in['gate_w'], 'L0_ffn_w1': _L0_ffn_in['w1'], 'L0_ffn_b1': _L0_ffn_in['b1'], 'L0_ffn_w2': _L0_ffn_in['w2'], 'L0_ffn_b2': _L0_ffn_in['b2'], 'L0_ffn_w3': _L0_ffn_in['w3'], 'L0_ffn_b3': _L0_ffn_in['b3'], 'L0_ffn_sw1': _L0_ffn_in['sw1'], 'L0_ffn_sb1': _L0_ffn_in['sb1'], 'L0_ffn_sw2': _L0_ffn_in['sw2'], 'L0_ffn_sb2': _L0_ffn_in['sb2'], 'L0_ffn_sw3': _L0_ffn_in['sw3'], 'L0_ffn_sb3': _L0_ffn_in['sb3'], 'L1_ffn_gate_w': _L1_ffn_in['gate_w'], 'L1_ffn_wg': _L1_ffn_in['wg'], 'L1_ffn_wu': _L1_ffn_in['wu'], 'L1_ffn_wd': _L1_ffn_in['wd'], 'L1_ffn_sg': _L1_ffn_in['sg'], 'L1_ffn_su': _L1_ffn_in['su'], 'L1_ffn_sd': _L1_ffn_in['sd']}

def reference(x, ctx_2048, mask_BxS2_bk0, L0_xattn_W_q, L0_xattn_W_k, L0_xattn_W_v, L0_xattn_W_o, L0_ffn_gate_w, L0_ffn_w1, L0_ffn_b1, L0_ffn_w2, L0_ffn_b2, L0_ffn_w3, L0_ffn_b3, L0_ffn_sw1, L0_ffn_sb1, L0_ffn_sw2, L0_ffn_sb2, L0_ffn_sw3, L0_ffn_sb3, L1_ffn_gate_w, L1_ffn_wg, L1_ffn_wu, L1_ffn_wd, L1_ffn_sg, L1_ffn_su, L1_ffn_sd):
    import jax
    import jax.numpy as jnp

    def _L0_xattn_ref(X_Query, X_Key, X_Value, W_q, W_k, W_v, W_o):
        import jax, jax.numpy as jnp
        import numpy as np
        NUM_HEADS = 8

        def _proj(W, x):
            return jnp.einsum('oi,bin->bon', W, x)

        def _split_heads(x, h):
            B, D, N = x.shape
            return x.reshape(B, D, h, N // h).transpose(2, 0, 1, 3)

        def _mha(XQ, XK, XV, Wq, Wk, Wv, Wo):
            B, D, N = XQ.shape
            h = NUM_HEADS
            Nh = N // h
            q = _split_heads(_proj(Wq, XQ), h)
            k = _split_heads(_proj(Wk, XK), h)
            v = _split_heads(_proj(Wv, XV), h)
            scores = jnp.einsum('hbdn,hben->hbde', q, k) / jnp.sqrt(jnp.asarray(Nh, q.dtype))
            p = jax.nn.softmax(scores, axis=-1)
            out = jnp.einsum('hbde,hben->hbdn', p, v)
            attn_heads = out.transpose(1, 2, 0, 3).reshape(B, D, N)
            return _proj(Wo, XQ - attn_heads)
        return _mha(X_Query, X_Key, X_Value, W_q, W_k, W_v, W_o)

    def _L0_ffn_ref(x, gate_w, w1, b1, w2, b2, w3, b3, sw1, sb1, sw2, sb2, sw3, sb3):
        import jax, jax.numpy as jnp
        import numpy as np
        E, K, D, INTER, SH_INTER = (16, 2, 256, 176, 352)
        ROUTE_SCALE = 1.0

        def _moe_forward(x, gate_w, w1, b1, w2, b2, w3, b3, sw1, sb1, sw2, sb2, sw3, sb3):
            shape = x.shape
            xt = x.reshape(-1, shape[-1])
            T = xt.shape[0]
            probs = jax.nn.softmax((xt @ gate_w.T).astype(jnp.float32), axis=-1)
            topw, topi = jax.lax.top_k(probs, K)
            weights = (topw * ROUTE_SCALE).astype(x.dtype)
            cw = jnp.zeros((T, E), x.dtype).at[jnp.arange(T)[:, None], topi].add(weights)

            def step(acc, p):
                W1, B1, W2, B2, W3, B3, wcol = p
                h = jax.nn.silu(xt @ W1.T + B1) * (xt @ W3.T + B3)
                return (acc + wcol[:, None] * (h @ W2.T + B2), None)
            y, _ = jax.lax.scan(step, jnp.zeros_like(xt), (w1, b1, w2, b2, w3, b3, cw.T))
            z = jax.nn.silu(xt @ sw1.T + sb1) * (xt @ sw3.T + sb3) @ sw2.T + sb2
            return (y + z).reshape(shape)
        return _moe_forward(x, gate_w, w1, b1, w2, b2, w3, b3, sw1, sb1, sw2, sb2, sw3, sb3)

    def _L1_xattn_ref(hidden_states, memory_tokens, memory_mask):
        import jax, jax.numpy as jnp
        import numpy as np
        B, S, D = hidden_states.shape
        scale = 1.0 / jnp.sqrt(jnp.asarray(D, hidden_states.dtype))
        scores = jnp.einsum('bsd,bmd->bsm', hidden_states, memory_tokens) * scale
        neg_inf = jnp.asarray(-1e+30, scores.dtype)
        scores = jnp.where(memory_mask[:, None, :], scores, neg_inf)
        attn = jax.nn.softmax(scores, axis=-1)
        readout = jnp.einsum('bsm,bmd->bsd', attn, memory_tokens)
        valid_b = jnp.any(memory_mask, axis=-1)
        out = jnp.where(valid_b[:, None, None], readout, jnp.zeros_like(readout))
        return out

    def _L1_ffn_ref(hidden_states, gate_w, wg, wu, wd, sg, su, sd):
        import jax, jax.numpy as jnp
        import numpy as np
        HID = 256
        N_EXP = 32
        F_EXP = 96
        TOP_K = 6
        F_SH = 192
        B, S = (1, 128)
        orig_shape = hidden_states.shape
        x = hidden_states.reshape(-1, HID)
        scores = jax.nn.sigmoid(x @ gate_w)
        topk_w, topk_i = jax.lax.top_k(scores, TOP_K)
        topk_w = topk_w / (jnp.sum(topk_w, axis=-1, keepdims=True) + 1e-20)
        combine = jnp.sum(jax.nn.one_hot(topk_i, N_EXP, dtype=topk_w.dtype) * topk_w[..., None], axis=1)
        g = jnp.einsum('td,edf->tef', x, wg)
        u = jnp.einsum('td,edf->tef', x, wu)
        act = jax.nn.silu(g) * u
        routed = jnp.einsum('tef,efd,te->td', act, wd, combine)
        routed = routed.reshape(orig_shape)
        shared = jax.nn.silu(hidden_states @ sg) * (hidden_states @ su) @ sd
        return routed + shared
    x = x + _L0_xattn_ref(_layernorm(x, axis=-1), ctx_2048, ctx_2048, L0_xattn_W_q, L0_xattn_W_k, L0_xattn_W_v, L0_xattn_W_o)
    x = x + _L0_ffn_ref(_layernorm(x, axis=-1), L0_ffn_gate_w, L0_ffn_w1, L0_ffn_b1, L0_ffn_w2, L0_ffn_b2, L0_ffn_w3, L0_ffn_b3, L0_ffn_sw1, L0_ffn_sb1, L0_ffn_sw2, L0_ffn_sb2, L0_ffn_sw3, L0_ffn_sb3)
    x = x + _L1_xattn_ref(_layernorm(x, axis=-1), ctx_2048, mask_BxS2_bk0)
    x = x + _L1_ffn_ref(_layernorm(x, axis=-1), L1_ffn_gate_w, L1_ffn_wg, L1_ffn_wu, L1_ffn_wd, L1_ffn_sg, L1_ffn_su, L1_ffn_sd)
    return x

_drawn_inputs = setup_inputs


def setup_inputs(seed=0):
    import zlib

    import numpy as np

    out = dict(_drawn_inputs(seed))
    spreads = {}
    factors = {'L0_ffn_gate_w': 8.0,
     'L0_ffn_w1': 8.0,
     'L0_ffn_b1': 8.0,
     'L0_ffn_w2': 8.0,
     'L0_ffn_b2': 8.0,
     'L0_ffn_w3': 8.0,
     'L0_ffn_b3': 8.0,
     'L0_ffn_sw1': 4.486,
     'L0_ffn_sb1': 8.0,
     'L0_ffn_sw2': 4.414,
     'L0_ffn_sb2': 4.354,
     'L0_ffn_sw3': 4.417,
     'L0_ffn_sb3': 8.0,
     'L1_ffn_gate_w': 8.0,
     'L1_ffn_wg': 8.0,
     'L1_ffn_wu': 8.0,
     'L1_ffn_wd': 8.0,
     'L1_ffn_sg': 6.37,
     'L1_ffn_su': 6.221,
     'L1_ffn_sd': 6.206}
    for name, (base, spread) in spreads.items():
        noise = np.random.default_rng([zlib.crc32(name.encode()), seed]).standard_normal(out[name].shape)
        drawn = base * np.exp(spread * noise) if base else spread * noise
        out[name] = jnp.asarray(drawn.astype(out[name].dtype))
    for name, factor in factors.items():
        out[name] = (out[name] * factor).astype(out[name].dtype)
    return out
```

```python
import concourse.bass as bass
from concourse import mybir
from contextlib import ExitStack

F32 = mybir.dt.float32
BF16 = mybir.dt.bfloat16
U32 = mybir.dt.uint32
I32 = mybir.dt.int32
U8 = mybir.dt.uint8
ALU = mybir.AluOpType
ACT = mybir.ActivationFunctionType
AX_X = mybir.AxisListType.X

P = 128
B, S, D = 32, 64, 256
TOKENS = B * S
NT = TOKENS // P
DC = D // P
HEADS, HD = 8, 32
HC = HEADS // DC
EPS = 1e-5
DEST = D
WEIGHT = D + 1
ROW = D + 2
LIST = TOKENS + P
RING = 8

class Layer:

    def __init__(self, n, experts, top, f, fchunk, bias, shared, fs):
        self.n, self.experts, self.top, self.f, self.fchunk = n, experts, top, f, fchunk
        self.bias = bias
        self.shared, self.fs = shared, fs
        self.tiles = TOKENS * top // P + experts
        self.zero_row = experts * LIST
        self.list_rows = self.zero_row + P
        self.out_rows = TOKENS * top


LAYERS = [
    Layer(n=0, experts=16, top=2, f=176, fchunk=88, bias=True, shared=[(0, 128), (128, 128), (256, 96)], fs=352),
    Layer(n=1, experts=32, top=6, f=96, fchunk=96, bias=False, shared=[(0, 96), (96, 96)], fs=192),
]


class Memory:
    pass


def exists(tile, count):
    return not isinstance(tile, int) or 0 <= tile < count


def wait_reuse(eng, sem, tile, lag, each=1):
    if not isinstance(tile, int) or tile - lag >= 0:
        eng.wait_ge(sem, (tile - lag + 1) * each)


def hold(eng, m):
    eng.sem_inc(m.s_held, 1)


def pipeline(eng, step, tiles, unroll, lead, lag):
    first = unroll + lag
    rounds = (tiles - lead - first) // unroll
    for i in range(-lead, first):
        step(i // unroll, i % unroll)
    with eng.Fori(1, 1 + rounds) as u:
        for j in range(lag, lag + unroll):
            step(u, j)
    for i in range(first + rounds * unroll, tiles + lag):
        step(i // unroll, i % unroll)


def shifted(u, j, by, unroll):
    return u + (j + by) // unroll, (j + by) % unroll


class Phase:

    def __init__(self, nc):
        self.nc, self.taken = nc, []

    def take(self, name):
        self.taken.append(self.nc.alloc_semaphore(name))
        return self.taken[-1]

    def end(self):
        self.nc.clear_and_free_semaphores(self.taken)
        self.nc.all_engine_barrier()
        self.taken = []


def program(nc, a, out):
    ctx = ExitStack()
    with ctx:
        def sb(name, shape, dt=F32):
            return ctx.enter_context(nc.sbuf_tensor(name, shape, dt))

        def sem(name):
            return nc.alloc_semaphore(name)

        m = Memory()
        m.phase = Phase(nc)
        m.x = sb("x_all", [P, NT, D])
        m.hT = sb("hT_all", [P, DC, TOKENS])
        m.w_in = sb("w_in", [P, DC, 32 * 192])
        m.w_out = sb("w_out", [96, 32 * D])
        m.wq = sb("wq", [P, P])
        m.wk = sb("wk", [P, P])
        m.wv = sb("wv", [P, 2, P])
        m.wo = sb("wo", [P, P])
        m.gate = [sb("gate0", [P, DC, 16]), sb("gate1", [P, DC, 32])]
        m.sw_in = [sb("sw_in0", [P, DC, 704]), sb("sw_in1", [P, DC, 384])]
        m.sw_out = [sb("sw_out0", [P, 3, D]), sb("sw_out1", [96, 2, D])]
        m.sbias = sb("sbias", [P, 3, 2])
        m.b2 = sb("b2", [17, D])
        m.mask8 = sb("mask8", [P, NT, S], U8)
        m.ident = sb("ident", [P, P])
        m.upper = sb("upper", [P, P], BF16)
        m.ones = sb("ones", [P, P], BF16)
        m.iota_p = sb("iota_p", [P, 1])
        m.eps = sb("eps_c", [P, 1])
        m.mhalf = sb("mhalf", [P, 1])
        m.iota_e = [sb("iota_e0", [P, 2, 16]), sb("iota_e1", [P, 6, 32])]
        m.list0 = [sb("list0_0", [P, 16]), sb("list0_1", [P, 32])]
        m.dest = [sb("dest0", [P, NT, 2], I32), sb("dest1", [P, NT, 6], I32)]
        m.zrow = [sb("zrow0", [P, ROW]), sb("zrow1", [P, ROW])]
        m.tab = sb("tab", [1, 3, P], I32)
        m.cw = sb("cw", [P, NT, 17])
        m.bank = [ctx.enter_context(nc.psum_tensor(f"bank{i}", [P, 512], F32)) for i in range(8)]
        m.lists = [nc.dram_tensor(f"lists{l.n}", (l.list_rows, ROW), F32, kind="Internal").ap() for l in LAYERS]
        m.res = [nc.dram_tensor(f"results{l.n}", (l.out_rows, D), F32, kind="Internal").ap() for l in LAYERS]

        m.sem_weights = [sem("loaded_moe0"), sem("loaded_moe1")]
        m.sem_small = sem("loaded_small")
        m.s_held = sem("waits_ended")
        m.sem_zero_lists = sem("zero_lists")

        setup(nc, m, a)
        m.phase.end()
        attend_heads(nc, m, a)
        m.phase.end()
        with nc.sbuf_tensor("bias_in", [P, 16 * 352], F32) as m.bias_in:
            shared_alone(nc, m, a, LAYERS[0])
            m.phase.end()
            experts(nc, m, LAYERS[0])
            m.phase.end()
        attend_masked(nc, m, a)
        m.phase.end()
        experts(nc, m, LAYERS[1])
        m.phase.end()
        finish(nc, m, out)


def load_experts(eng, m, a, l):
    s = m.sem_weights[l.n]
    w_in, w_out = (a["w13"], a["w2"]) if l.n == 0 else (a["wgu"], a["wd"])
    n = l.experts * 2 * l.f
    quarter = n // 4
    for q in range(4):
        eng.dma_start(m.w_in[:, :, q * quarter:(q + 1) * quarter],
                      w_in.rearrange("(c p) n -> p c n", p=P)[:, :, q * quarter:(q + 1) * quarter]).then_inc(s, 16)
    eng.dma_start(w_out_view(m, l), w_out.rearrange("(c p) n -> p c n", p=l.fchunk)).then_inc(s, 16)


def w_out_view(m, l):
    return m.w_out[0:l.fchunk, :].rearrange("p (c n) -> p c n", c=l.f // l.fchunk)


def setup(nc, m, a):
    ctx = ExitStack()
    with ctx:
        def sem(name):
            return m.phase.take(name)
        s_x, s_att = sem("loaded_x"), sem("loaded_attention")
        s_zero, s_made = sem("zeroed"), sem("constants_made")
        s_zrow = sem("zero_rows_made")
        it = ctx.enter_context(nc.sbuf_tensor("iota_tmp", [P, 6 * 32 + 1], I32))
        with nc.Block() as block:

            @block.sync
            def _(sp):
                sp.wait_ge(s_zero, 1)
                for half in range(2):
                    r = slice(64 * half, 64 * half + 64)
                    for w, src in ((m.wq, a["wqT"]), (m.wk, a["wkT"]), (m.wo, a["woT"])):
                        sp.dma_start(w[r, r], src).then_inc(s_att, 16)
                    for dup in range(2):
                        sp.dma_start(m.wv[r, half, 64 * dup:64 * dup + 64], a["wvT"]).then_inc(s_att, 16)
                for q in range(4):
                    t = slice(4 * q, 4 * q + 4)
                    sp.dma_start(m.x[:, t, :], a["x"].rearrange("(t p) d -> p t d", p=P)[:, t, :]).then_inc(s_x, 16)
                sp.wait_ge(s_att, 10 * 16)
                sp.wait_ge(s_x, 4 * 16)

            @block.scalar
            def _(act):
                small = [(m.gate[n][:, :, :], g.rearrange("(c p) e -> p c e", p=P)) for n, g in ((0, a["gate0"]), (1, a["gate1"]))]
                small += [(m.b2[:, :], a["b2aug"])]
                small += [(m.sbias[0:fs, c, k:k + 1], b.rearrange("(f o) -> f o", o=1)[f0:f0 + fs, :]) for c, (f0, fs) in enumerate(LAYERS[0].shared)
                          for k, b in ((0, a["sb1"]), (1, a["sb3"]))]
                small += [(m.sw_in[n][:, :, :], w.rearrange("(c p) n -> p c n", p=P)) for n, w in ((0, a["sw13"]), (1, a["sgu"]))]
                small += [(m.sw_out[0][0:fs, c, :], a["sw2"][f0:f0 + fs, :]) for c, (f0, fs) in enumerate(LAYERS[0].shared)]
                small += [(m.sw_out[1][:, :, :], a["sd"].rearrange("(c p) n -> p c n", p=96))]
                small += [(m.mask8[64 * h:64 * h + 64, :, :],
                           a["mask"].rearrange("(t h) s -> h t s", h=2)[h:h + 1, :, :].to_broadcast([64, NT, S])) for h in range(2)]
                m.small_count = 16 * len(small)
                for dst, src in small:
                    act.dma_start(dst, src).then_inc(m.sem_small, 16)
                act.wait_ge(s_zrow, 4)
                for l in LAYERS:
                    act.dma_start(m.lists[l.n][l.zero_row:l.zero_row + P, :], m.zrow[l.n][:, :]).then_inc(m.sem_zero_lists, 16)
                load_experts(act, m, a, LAYERS[0])
                act.wait_ge(m.sem_small, m.small_count)

            @block.gpsimd
            def _(pool):
                g = nc.gpsimd
                made = [0]

                def then(op):
                    made[0] += 1
                    op.then_inc(s_made, 1)
                    pool.wait_ge(s_made, made[0])

                for l in LAYERS:
                    g.iota(m.zrow[l.n][:, DEST:DEST + 1].bitcast(I32), pattern=[[1, 1]], base=l.out_rows,
                           channel_multiplier=1).then_inc(s_zrow, 1)
                g.memset(m.eps[:, :], EPS)
                g.memset(m.mhalf[:, :], -0.5)
                g.memset(m.ident[:, :], 0.0)
                g.memset(m.ones[:, :], 1.0)
                then(g.memset(m.upper[:, :], 1.0))
                g.affine_select(out=m.ident[:, :], in_=m.ident[:, :], compare_op=ALU.not_equal, fill=1.0,
                                base=0, pattern=[[-1, P]], channel_multiplier=1)
                g.affine_select(out=m.upper[:, :], in_=m.upper[:, :], compare_op=ALU.is_gt, fill=0.0,
                                base=0, pattern=[[1, P]], channel_multiplier=-1)
                then(g.iota(it[:, 192:193], pattern=[[1, 1]], base=0, channel_multiplier=1))
                then(g.tensor_copy(m.iota_p[:, :], it[:, 192:193]))
                for l in LAYERS:
                    k, e = l.top, l.experts
                    g.iota(m.dest[l.n][:, :, :], pattern=[[P * k, NT], [1, k]], base=0, channel_multiplier=k)
                    numbers = it[:, 0:k * e].rearrange("p (k e) -> p k e", k=k)
                    then(g.iota(numbers, pattern=[[0, k], [1, e]], base=0, channel_multiplier=0))
                    g.tensor_copy(m.iota_e[l.n][:, :, :], numbers)
                    then(g.tensor_scalar(m.list0[l.n][:, :], numbers[:, 0, :], float(LIST), 0.0, ALU.mult, ALU.add))

            @block.vector
            def _(dve):
                v = nc.vector
                for w in (m.wq[:, :], m.wk[:, :], m.wo[:, :]):
                    v.memset(w, 0.0)
                v.memset(m.wv[:, :, :], 0.0)
                for l in LAYERS:
                    v.memset(m.zrow[l.n][:, 0:D], 0.0)
                    v.memset(m.zrow[l.n][:, WEIGHT:ROW], 0.0).then_inc(s_zrow, 1)
                v.memset(m.cw[:, :, 16:17], 1.0).then_inc(s_zero, 1)


class Norm:

    def __init__(self, nc, ctx, m, name):
        sb = lambda n, w: ctx.enter_context(nc.sbuf_tensor(f"{name}_{n}", [P, 2, w], F32))
        sem = lambda n: m.phase.take(f"{name}_{n}")
        self.stats, self.mv, self.rstd = sb("stats", 6), sb("mean_var", 2), sb("rstd", 1)
        self.out = sb("out", D)
        self.s_stats, self.s_mv, self.s_var, self.s_rstd, self.s_out = (
            sem("stats_done"), sem("mean_var_done"), sem("var_eps_done"), sem("rstd_done"), sem("normed"))


def norm_stats(nc, dve, m, n, x, t, b):
    hold(dve, m)
    nc.vector.bn_stats(n.stats[:, b, :], x).then_inc(n.s_stats, 1)
    dve.wait_ge(n.s_stats, t + 1)
    hold(dve, m)
    nc.vector.bn_aggr(n.mv[:, b, :], n.stats[:, b, :]).then_inc(n.s_mv, 1)


def norm_rstd(nc, pool, m, n, t, b):
    pool.wait_ge(n.s_mv, t + 1)
    nc.gpsimd.tensor_tensor(n.rstd[:, b, :], n.mv[:, b, 1:2], m.eps[:, :], ALU.add).then_inc(n.s_var, 1)
    pool.wait_ge(n.s_var, t + 1)
    nc.gpsimd.tensor_tensor(n.rstd[:, b, :], n.rstd[:, b, :], m.mhalf[:, :], ALU.pow).then_inc(n.s_rstd, 1)


def norm_apply(nc, dve, n, x, t, b):
    dve.wait_ge(n.s_mv, t + 1)
    dve.wait_ge(n.s_rstd, t + 1)
    nc.vector.tensor_scalar(n.out[:, b, :], x, n.mv[:, b, 0:1], n.rstd[:, b, :], ALU.subtract, ALU.mult).then_inc(n.s_out, 1)


class Router:

    def __init__(self, nc, ctx, m, l, bank):
        e, k = l.experts, l.top
        name = f"route{l.n}"
        sb = lambda n, shape, dt=F32: ctx.enter_context(nc.sbuf_tensor(f"{name}_{n}", [P, 2] + shape, dt))
        sem = lambda n: m.phase.take(f"{name}_{n}")
        self.l, self.bank = l, bank
        self.logits_ps = bank[:, 256:256 + e]
        self.rank_ps = bank[:, 320:320 + e]
        self.count_ps = bank[:, 384:384 + e]
        self.hT = sb("hT", [DC, P])
        self.lg, self.top, self.negm = sb("logits", [e]), sb("top8", [8]), sb("neg_max", [1])
        self.idx = sb("index8", [8], U32)
        self.oh = sb("onehot", [k, e])
        self.sel = sb("chosen", [e], BF16)
        self.cum = ctx.enter_context(nc.sbuf_tensor(f"{name}_chosen_before", [P, e], BF16))
        self.place, self.prod = sb("place", [e]), sb("place_of_choice", [k, e])
        self.slot = sb("slot", [k], U32)
        self.cwk = sb("weight_of_choice", [2, 16])
        self.ex, self.sum, self.rs = sb("exps", [e]), sb("sum", [1]), sb("rsum", [1])
        self.ew, self.wt = sb("top_exps", [k]), sb("weights", [k])
        self.pay = sb("rows", [k, ROW])
        self.s_hT_ps, self.s_hT_sb, self.s_logits, self.s_lg, self.s_top, self.s_negm = sem("hT_ps"), sem("hT_sb"), sem("logits"), sem("lg"), sem("top"), sem("negm")
        self.s_idx, self.s_oh, self.s_sel, self.s_cum, self.s_rank, self.s_place = sem("idx"), sem("oh"), sem("sel"), sem("cum"), sem("rank"), sem("place")
        self.s_prod, self.s_slot, self.s_exps, self.s_w1, self.s_w2, self.s_w3 = sem("prod"), sem("slot"), sem("exps"), sem("w1"), sem("w2"), sem("w3")
        self.s_w4, self.s_weights, self.s_cwprod, self.s_cw, self.s_rows, self.s_dest = sem("w4"), sem("weights"), sem("cwprod"), sem("cw"), sem("rows"), sem("dest")
        self.s_sent = [sem("sent_even"), sem("sent_odd")]
        self.s_kept = [sem("hT_kept_even"), sem("hT_kept_odd")]
        self.s_counts, self.s_tab, self.s_rows_ps, self.s_tables = sem("counts"), sem("table_steps"), sem("table_rows_ps"), sem("tables")
        self.s_tail = sem("tails_zeroed")
        tb = lambda n, shape, dt=F32: ctx.enter_context(nc.sbuf_tensor(f"{name}_{n}", shape, dt))
        self.nf, self.ni, self.ti, self.tf = tb("n", [P, e]), tb("n_int", [P, e], I32), tb("tiles_int", [P, e], I32), tb("tiles", [P, e])
        self.ends, self.le, self.step, self.ls = tb("ends", [P, e]), tb("le", [P, e]), tb("step", [P, e]), tb("le_step", [P, e])
        self.onesf = tb("ones", [P, e])
        self.col = tb("col", [P, 4])


def router_pe_transpose(nc, pe, m, r, h, s_h, t, b):
    pe.wait_ge(s_h, t + 1)
    wait_reuse(pe, r.s_hT_sb, t, 1)
    wait_reuse(pe, r.s_lg, t, 1)
    wait_reuse(pe, r.s_place, t, 1)
    for c in range(DC):
        last = nc.tensor.transpose(r.bank[:, c * P:(c + 1) * P], h[:, b, c * P:(c + 1) * P], m.ident[:, :])
    last.then_inc(r.s_hT_ps, 1)


def router_act_hT(nc, act, m, r, t, b, u):
    act.wait_ge(r.s_hT_ps, t + 1)
    wait_reuse(act, r.s_logits, t, 2)
    if not isinstance(t, int) or t >= 2:
        act.wait_ge(r.s_kept[b], u * 16)
    nc.scalar.activation(r.hT[:, b, :, :], r.bank[:, 0:D].rearrange("p (c n) -> p c n", c=DC), ACT.Copy).then_inc(r.s_hT_sb, 1)


def router_sp_keep(nc, sp, m, r, t, b):
    sp.wait_ge(r.s_hT_sb, t + 1)
    sp.dma_start(m.hT[:, :, bass.ds(t * P, P)], r.hT[:, b, :, :]).then_inc(r.s_kept[b], 16)


def router_pe_logits(nc, pe, m, r, t, b):
    pe.wait_ge(r.s_hT_sb, t + 1)
    for c in range(DC):
        last = nc.tensor.matmul(r.logits_ps, r.hT[:, b, c, :], m.gate[r.l.n][:, c, :], start=(c == 0), stop=(c == DC - 1))
    last.then_inc(r.s_logits, 1)


def router_dve_choose(nc, dve, m, r, t, b):
    v, l = nc.vector, r.l
    e, k = l.experts, l.top
    dve.wait_ge(r.s_logits, t + 1)
    wait_reuse(dve, r.s_exps, t, 2)
    v.tensor_copy(r.lg[:, b, :], r.logits_ps).then_inc(r.s_lg, 1)
    dve.wait_ge(r.s_lg, t + 1)
    hold(dve, m)
    v.max(r.top[:, b, :], r.lg[:, b, :]).then_inc(r.s_top, 1)
    dve.wait_ge(r.s_top, t + 1)
    hold(dve, m)
    v.max_index(r.idx[:, b, :], r.top[:, b, :], r.lg[:, b, :]).then_inc(r.s_idx, 1)
    v.tensor_scalar(r.negm[:, b, :], r.top[:, b, 0:1], -1.0, None, ALU.mult).then_inc(r.s_negm, 1)
    dve.wait_ge(r.s_idx, t + 1)
    v.tensor_tensor(r.oh[:, b, :, :], m.iota_e[l.n][:, :, :], r.idx[:, b, 0:k].unsqueeze(2).to_broadcast([P, k, e]), ALU.is_equal).then_inc(r.s_oh, 1)
    dve.wait_ge(r.s_oh, t + 1)
    with nc.allow_low_precision("sums of ones"):
        v.tensor_reduce(r.sel[:, b, :], r.oh[:, b, :, :].rearrange("p k e -> p e k"), AX_X, ALU.add).then_inc(r.s_sel, 1)


def router_act_exps(nc, act, m, r, t, b):
    l = r.l
    act.wait_ge(r.s_negm, t + 1)
    wait_reuse(act, r.s_weights, t, 2)
    if l.n == 0:
        nc.scalar.activation(r.ex[:, b, :], r.lg[:, b, :], ACT.Exp, bias=r.negm[:, b, :], accum_out=r.sum[:, b, :])
        nc.scalar.activation(r.ew[:, b, :], r.top[:, b, 0:l.top], ACT.Exp, bias=r.negm[:, b, :]).then_inc(r.s_exps, 1)
    else:
        nc.scalar.activation(r.ew[:, b, :], r.top[:, b, 0:l.top], ACT.Exp, scale=-1.0).then_inc(r.s_exps, 1)


def router_pe_rank(nc, pe, m, r, t, b):
    pe.wait_ge(r.s_sel, t + 1)
    pe.wait_ge(r.s_cum, t + 1)
    nc.tensor.matmul(r.rank_ps, m.upper[:, :], r.sel[:, b, :], start=True, stop=False)
    nc.tensor.matmul(r.rank_ps, m.ones[:, :], r.cum[:, :], start=False, stop=True).then_inc(r.s_rank, 1)


def router_dve_place(nc, dve, m, r, t, b, u):
    v, l = nc.vector, r.l
    e, k = l.experts, l.top
    dve.wait_ge(r.s_rank, t + 1)
    v.tensor_tensor(r.place[:, b, :], r.rank_ps, m.list0[l.n][:, :], ALU.add).then_inc(r.s_place, 1)
    with nc.allow_low_precision("counts up to the number of tiles"):
        v.tensor_tensor(r.cum[:, :], r.cum[:, :], r.sel[:, b, :], ALU.add).then_inc(r.s_cum, 1)
    dve.wait_ge(r.s_place, t + 1)
    v.tensor_tensor(r.prod[:, b, :, :], r.oh[:, b, :, :], r.place[:, b, :].unsqueeze(1).to_broadcast([P, k, e]), ALU.mult).then_inc(r.s_prod, 1)
    dve.wait_ge(r.s_exps, t + 1)
    if l.n == 0:
        v.reciprocal(r.rs[:, b, :], r.sum[:, b, :]).then_inc(r.s_w1, 1)
    else:
        v.tensor_scalar(r.wt[:, b, :], r.ew[:, b, :], 1.0, None, ALU.add).then_inc(r.s_w1, 1)
    dve.wait_ge(r.s_prod, t + 1)
    if not isinstance(t, int) or t >= 2:
        dve.wait_ge(r.s_sent[b], u * (16 * k))
    with nc.allow_low_precision("whole numbers"):
        v.tensor_reduce(r.slot[:, b, :], r.prod[:, b, :, :], AX_X, ALU.add).then_inc(r.s_slot, 1)
    v.tensor_copy(r.pay[:, b, :, DEST:DEST + 1].bitcast(I32), m.dest[l.n][:, bass.ds(t, 1), :].rearrange("p o k -> p k o")).then_inc(r.s_dest, 1)
    dve.wait_ge(r.s_w1, t + 1)
    w_out = r.pay[:, b, :, WEIGHT:ROW].rearrange("p k o -> p (k o)")
    if l.n == 0:
        v.tensor_scalar(w_out, r.ew[:, b, :], r.rs[:, b, :], None, ALU.mult).then_inc(r.s_weights, 1)
        dve.wait_ge(r.s_weights, t + 1)
        for c in range(k):
            last = v.tensor_scalar(r.cwk[:, b, c, :], r.oh[:, b, c, :], r.pay[:, b, c, WEIGHT:ROW], None, ALU.mult)
        last.then_inc(r.s_cwprod, 1)
        dve.wait_ge(r.s_cwprod, t + 1)
        v.tensor_tensor(m.cw[:, bass.ds(t, 1), 0:e].rearrange("p o e -> p (o e)"), r.cwk[:, b, 0, :], r.cwk[:, b, 1, :], ALU.add).then_inc(r.s_cw, 1)
    else:
        v.reciprocal(r.wt[:, b, :], r.wt[:, b, :]).then_inc(r.s_w2, 1)
        dve.wait_ge(r.s_w2, t + 1)
        v.tensor_reduce(r.sum[:, b, :], r.wt[:, b, :], AX_X, ALU.add).then_inc(r.s_w3, 1)
        dve.wait_ge(r.s_w3, t + 1)
        v.tensor_scalar(r.sum[:, b, :], r.sum[:, b, :], 1e-20, None, ALU.add).then_inc(r.s_w4, 1)
        dve.wait_ge(r.s_w4, t + 1)
        v.reciprocal(r.rs[:, b, :], r.sum[:, b, :]).then_inc(r.s_cwprod, 1)
        dve.wait_ge(r.s_cwprod, t + 1)
        v.tensor_scalar(w_out, r.wt[:, b, :], r.rs[:, b, :], None, ALU.mult).then_inc(r.s_weights, 1)


def router_act_rows(nc, act, m, r, h, t, b, u):
    k = r.l.top
    if not isinstance(t, int) or t >= 2:
        act.wait_ge(r.s_sent[b], u * (16 * k))
    nc.scalar.activation(r.pay[:, b, :, 0:D], h[:, b, :].unsqueeze(1).to_broadcast([P, k, D]), ACT.Copy).then_inc(r.s_rows, 1)


def router_pool_send(nc, pool, m, r, t, b):
    pool.wait_ge(r.s_rows, t + 1)
    pool.wait_ge(r.s_weights, t + 1)
    pool.wait_ge(r.s_slot, t + 1)
    pool.wait_ge(r.s_dest, t + 1)
    hold(pool, m)
    for k in range(r.l.top):
        pool.indirect_dma_start(m.lists[r.l.n][:, :], bass.IndirectOffsetOnAxis(ap=r.slot[:, b, k:k + 1], axis=0),
                                r.pay[:, b, k, :], None).then_inc(r.s_sent[b], 16)


def router_pe_tables(nc, pe, m, r):
    pe.wait_ge(r.s_cum, NT + 1)
    pe.wait_ge(r.s_place, NT)
    nc.tensor.matmul(r.count_ps, m.ones[:, :], r.cum[:, :], start=True, stop=True).then_inc(r.s_counts, 1)
    pe.wait_ge(r.s_tab, 12)
    for n in range(2):
        last = nc.tensor.matmul(r.bank[0:1, n * P:(n + 1) * P], r.col[:, n:n + 1], m.ident[:, :], start=True, stop=True)
    last.then_inc(r.s_rows_ps, 1)


def router_dve_tables(nc, dve, m, r):
    v, l = nc.vector, r.l
    e = l.experts
    done = [0]

    def then(op):
        done[0] += 1
        op.then_inc(r.s_tab, 1)
        dve.wait_ge(r.s_tab, done[0])

    dve.wait_ge(r.s_counts, 1)
    then(v.memset(r.onesf[:, :], 1.0))
    then(v.tensor_copy(r.nf[:, :], r.count_ps))
    then(v.tensor_scalar(r.ni[:, :], r.nf[:, :], float(P - 1), None, ALU.add))
    then(v.tensor_scalar(r.ti[:, :], r.ni[:, :], P.bit_length() - 1, None, ALU.logical_shift_right))
    then(v.tensor_copy(r.tf[:, :], r.ti[:, :]))
    then(v.tensor_tensor_scan(r.ends[:, :], r.onesf[:, :], r.tf[:, :], 0.0, ALU.mult, ALU.add))
    then(v.tensor_scalar(r.le[:, :], r.ends[:, :], m.iota_p[:, :], None, ALU.is_le))
    then(v.tensor_scalar(r.step[:, :], r.tf[:, :], -float(P), float(LIST), ALU.mult, ALU.add))
    then(v.tensor_tensor(r.ls[:, :], r.le[:, :], r.step[:, :], ALU.mult))
    v.tensor_reduce(r.col[:, 2:3], r.le[:, :], AX_X, ALU.add)
    v.tensor_reduce(r.col[:, 3:4], r.ls[:, :], AX_X, ALU.add)
    then(v.tensor_tensor(m.tab[:, 2, 0:e], r.nf[0:1, :], m.list0[l.n][0:1, :], ALU.add))
    then(v.scalar_tensor_tensor(r.col[:, 1:2], m.iota_p[:, :], float(P), r.col[:, 3:4], ALU.mult, ALU.add))
    v.tensor_scalar(r.col[:, 0:1], r.col[:, 2:3], float(e - 1), None, ALU.min)
    then(v.tensor_scalar(r.col[:, 1:2], r.col[:, 1:2], float(l.zero_row), None, ALU.min))
    dve.wait_ge(r.s_rows_ps, 1)
    v.tensor_copy(m.tab[:, 0, :], r.bank[0:1, 0:P])
    v.tensor_copy(m.tab[:, 1, :], r.bank[0:1, P:2 * P]).then_inc(r.s_tables, 1)
    dve.wait_ge(r.s_tables, 1)


def router_sp_tails(nc, sp, m, r):
    l = r.l
    sp.wait_ge(r.s_tab, 10)
    with sp.Fori(0, l.experts) as e:
        row = sp.value_load(m.tab[0:1, 2, bass.ds(e, 1)], min_val=0, max_val=l.zero_row)
        sp.dma_start(m.lists[l.n][bass.ds(row, P), :], m.zrow[l.n][:, :]).then_inc(r.s_tail, 16)
    sp.wait_ge(r.s_tail, 16 * l.experts)


def tile_of(u, j, by, unroll=2):
    uu, jj = shifted(u, j, by, unroll)
    return uu * unroll + jj, jj, uu


def attend_heads(nc, m, a):
    l = LAYERS[0]
    ctx = ExitStack()
    with ctx:
        def sb(name, shape, dt=F32):
            return ctx.enter_context(nc.sbuf_tensor(name, shape, dt))

        def sem(name):
            return m.phase.take(name)

        q_ps, k_ps, v_ps, s_ps, pT_ps, o_ps, y_ps, h_ps = m.bank
        qn, hn = Norm(nc, ctx, m, "norm_q"), Norm(nc, ctx, m, "norm_h")
        r = Router(nc, ctx, m, l, h_ps)
        qT = sb("qT", [P, 2, DC, 2, S])
        kB = sb("kB", [P, 2, DC, 2, HC, S])
        vB = sb("vB", [P, 2, 2, HEADS // 2, 2 * HD + 2])
        sm, pr, pT = sb("scores", [P, 2, 512]), sb("probs", [P, 2, 512]), sb("probsT", [P, 2, 512])
        negmax, rec = sb("neg_row_max", [P, 2, HEADS]), sb("recip", [P, 2, HEADS])
        on, z = sb("attended", [P, 2, D]), sb("q_less_attended", [P, 2, D])

        ctxt = sb("context", [P, 2, D])
        s_init = sem("att_zeroed")
        s_ctx = [sem("context_even"), sem("context_odd")]
        s_qk, s_v = sem("qk_ps"), sem("v_ps")
        s_q_sb, s_k_sb, s_v_sb = sem("q_sb"), sem("k_sb"), sem("v_sb")
        s_sc, s_max, s_sub, s_exp = sem("scores_ps"), sem("row_max"), sem("scores_less_max"), sem("probs_done")
        s_pT, s_pT_sb, s_o, s_rec, s_on, s_z = sem("probsT_ps"), sem("probsT_sb"), sem("attended_ps"), sem("recip_done"), sem("attended_sb"), sem("z_done")
        s_y, s_x1 = sem("y_ps"), sem("x1_done")
        BH = P // HC

        with nc.Block() as block:

            @block.tensor
            def _(pe):
                mm = nc.tensor.matmul

                def project(t, b, u):
                    pe.wait_ge(s_ctx[b], u * 16 + 16)
                    pe.wait_ge(qn.s_out, t + 1)
                    wait_reuse(pe, s_q_sb, t, 1)
                    wait_reuse(pe, s_k_sb, t, 1)
                    for c in range(DC):
                        mm(q_ps[:, c * P:(c + 1) * P], qn.out[:, b, c * P:(c + 1) * P], m.wq[:, :], start=True, stop=True)
                        last = mm(k_ps[:, c * P:(c + 1) * P], ctxt[:, b, c * P:(c + 1) * P], m.wk[:, :], start=True, stop=True)
                    last.then_inc(s_qk, 1)
                    wait_reuse(pe, s_v_sb, t, 1)
                    for batch in range(2):
                        last = mm(v_ps[:, batch * D:(batch + 1) * D], m.wv[:, batch, :], ctxt[:, b, :], start=True, stop=True)
                    last.then_inc(s_v, 1)

                def scores(t, b):
                    pe.wait_ge(s_q_sb, t + 1)
                    pe.wait_ge(s_k_sb, t + 1)
                    wait_reuse(pe, s_sub, t, 1)
                    for batch in range(2):
                        for c in range(DC):
                            last = mm(s_ps[64 * batch:64 * batch + 64, c * 256:(c + 1) * 256], qT[:, b, c, batch, :],
                                      kB[:, b, c, batch, :, :], start=True, stop=True)
                    last.then_inc(s_sc, 1)

                def turn_probs(t, b):
                    pe.wait_ge(s_exp, t + 1)
                    wait_reuse(pe, s_pT_sb, t, 1)
                    for g in range(4):
                        last = nc.tensor.transpose(pT_ps[:, g * P:(g + 1) * P], pr[:, b, g * P:(g + 1) * P], m.ident[:, :])
                    last.then_inc(s_pT, 1)

                def attend(t, b):
                    pe.wait_ge(s_pT_sb, t + 1)
                    pe.wait_ge(s_v_sb, t + 1)
                    wait_reuse(pe, s_on, t, 1)
                    w = 2 * HD + 2
                    for batch in range(2):
                        for g in range(4):
                            last = mm(o_ps[64 * batch:64 * batch + 64, g * w:(g + 1) * w],
                                      pT[:, b, g * P + 64 * batch:g * P + 64 * batch + 64], vB[:, b, batch, g, :], start=True, stop=True)
                    last.then_inc(s_o, 1)

                def output(t, b):
                    pe.wait_ge(s_z, t + 1)
                    wait_reuse(pe, s_x1, t, 1)
                    mm(y_ps[:, 0:D], m.wo[:, :], z[:, b, :], start=True, stop=True).then_inc(s_y, 1)

                def step(u, j):
                    t, b, u0 = tile_of(u, j, 0)
                    t1, b1, _u = tile_of(u, j, -1)
                    t2, b2, _u = tile_of(u, j, -2)
                    if exists(t, NT):
                        project(t, b, u0)
                    if exists(t1, NT):
                        turn_probs(t1, b1)
                    if exists(t2, NT):
                        router_pe_transpose(nc, pe, m, r, hn.out, hn.s_out, t2, b2)
                    if exists(t1, NT):
                        attend(t1, b1)
                    if exists(t, NT):
                        scores(t, b)
                    if exists(t2, NT):
                        router_pe_logits(nc, pe, m, r, t2, b2)
                    if exists(t1, NT):
                        output(t1, b1)
                    if exists(t2, NT):
                        router_pe_rank(nc, pe, m, r, t2, b2)

                pe.wait_ge(s_init, 3)
                pipeline(pe, step, NT, 2, 0, 2)
                router_pe_tables(nc, pe, m, r)

            @block.scalar
            def _(act):
                copy = lambda o, i: nc.scalar.activation(o, i, ACT.Copy)

                def keep_qk(t, b):
                    act.wait_ge(s_qk, t + 1)
                    wait_reuse(act, s_sc, t, 2)
                    copy(qT[:, b, :, :, :], q_ps[:, 0:D].rearrange("p (c a s) -> p c a s", c=DC, a=2)).then_inc(s_q_sb, 1)
                    for h in range(HC):
                        rows = slice(BH * h, BH * h + BH)
                        last = copy(kB[rows, b, :, :, h, :], k_ps[rows, 0:D].rearrange("p (c a s) -> p c a s", c=DC, a=2))
                    last.then_inc(s_k_sb, 1)

                def keep_probsT(t, b):
                    act.wait_ge(s_pT, t + 1)
                    wait_reuse(act, s_o, t, 2)
                    copy(pT[:, b, :], pT_ps[:, :]).then_inc(s_pT_sb, 1)

                def exps(t, b):
                    act.wait_ge(s_sub, t + 1)
                    wait_reuse(act, s_pT, t, 2)
                    nc.scalar.activation(pr[:, b, :], sm[:, b, :], ACT.Exp, scale=float(HD) ** -0.5).then_inc(s_exp, 1)

                def step(u, j):
                    t, b, _u = tile_of(u, j, 0)
                    t1, b1, _u = tile_of(u, j, -1)
                    t2, b2, u2 = tile_of(u, j, -2)
                    if exists(t, NT):
                        keep_qk(t, b)
                    if exists(t1, NT):
                        keep_probsT(t1, b1)
                    if exists(t2, NT):
                        router_act_hT(nc, act, m, r, t2, b2, u2)
                    if exists(t, NT):
                        exps(t, b)
                    if exists(t2, NT):
                        router_act_exps(nc, act, m, r, t2, b2)
                        router_act_rows(nc, act, m, r, hn.out, t2, b2, u2)

                act.wait_ge(s_init, 3)
                pipeline(act, step, NT, 2, 0, 2)

            @block.gpsimd
            def _(pool):
                def step(u, j):
                    t, b, _u = tile_of(u, j, 1)
                    t1, b1, _u = tile_of(u, j, -1)
                    t2, b2, _u = tile_of(u, j, -2)
                    if exists(t1, NT):
                        norm_rstd(nc, pool, m, hn, t1, b1)
                    if exists(t, NT):
                        norm_rstd(nc, pool, m, qn, t, b)
                    if exists(t2, NT):
                        router_pool_send(nc, pool, m, r, t2, b2)

                pipeline(pool, step, NT, 2, 1, 2)
                for b in range(2):
                    pool.wait_ge(r.s_sent[b], 16 * l.top * NT // 2)

            @block.vector
            def _(dve):
                v = nc.vector

                def xt(t):
                    return m.x[:, bass.ds(t, 1), :].rearrange("p o n -> p (o n)")

                def keep_v(t, b):
                    dve.wait_ge(s_v, t + 1)
                    wait_reuse(dve, s_o, t, 2)
                    for par in range(2):
                        rows = slice(64 * par, 64 * par + 64)
                        src = v_ps[rows, :].rearrange("p (a g h n) -> p a g h n", a=2, g=4, h=2)[:, :, :, par, :]
                        last = v.tensor_copy(vB[rows, b, :, :, HD * par:HD * par + HD], src)
                    last.then_inc(s_v_sb, 1)

                def scores_less_max(t, b):
                    dve.wait_ge(s_sc, t + 1)
                    heads = s_ps[:, :].rearrange("p (h e) -> p h e", h=HEADS)
                    v.tensor_reduce(negmax[:, b, :], heads, AX_X, ALU.max, negate=True).then_inc(s_max, 1)
                    dve.wait_ge(s_max, t + 1)
                    wait_reuse(dve, s_exp, t, 2)
                    v.tensor_tensor(sm[:, b, :].rearrange("p (h e) -> p h e", h=HEADS), heads,
                                    negmax[:, b, :].unsqueeze(2).to_broadcast([P, HEADS, S]), ALU.add).then_inc(s_sub, 1)

                def subtract(t, b):
                    w = 2 * HD + 2
                    dve.wait_ge(s_o, t + 1)
                    o = o_ps[:, 0:4 * w].rearrange("p (g w) -> p g w", g=4)
                    v.reciprocal(rec[:, b, :].rearrange("p (g h) -> p g h", g=4), o[:, :, 2 * HD:w]).then_inc(s_rec, 1)
                    dve.wait_ge(s_rec, t + 1)
                    for par in range(2):
                        last = v.tensor_tensor(on[:, b, :].rearrange("p (g h n) -> p g h n", g=4, h=2)[:, :, par, :], o[:, :, HD * par:HD * par + HD],
                                               rec[:, b, :].rearrange("p (g h) -> p g h", g=4)[:, :, par:par + 1].to_broadcast([P, 4, HD]), ALU.mult)
                    last.then_inc(s_on, 1)
                    dve.wait_ge(s_on, t + 1)
                    wait_reuse(dve, s_y, t, 2)
                    v.tensor_tensor(z[:, b, :], qn.out[:, b, :], on[:, b, :], ALU.subtract).then_inc(s_z, 1)

                def residual(t, b):
                    dve.wait_ge(s_y, t + 1)
                    v.tensor_tensor(xt(t), y_ps[:, 0:D], xt(t), ALU.add).then_inc(s_x1, 1)
                    dve.wait_ge(s_x1, t + 1)
                    norm_stats(nc, dve, m, hn, xt(t), t, b)

                def step(u, j):
                    t0, b0, _u = tile_of(u, j, 1)
                    t, b, _u = tile_of(u, j, 0)
                    t1, b1, _u = tile_of(u, j, -1)
                    t2, b2, u2 = tile_of(u, j, -2)
                    if exists(t, NT):
                        keep_v(t, b)
                    if exists(t2, NT):
                        router_dve_choose(nc, dve, m, r, t2, b2)
                    if exists(t1, NT):
                        subtract(t1, b1)
                    if exists(t, NT):
                        scores_less_max(t, b)
                    if exists(t1, NT):
                        residual(t1, b1)
                    if exists(t2, NT):
                        router_dve_place(nc, dve, m, r, t2, b2, u2)
                    if exists(t1, NT):
                        wait_reuse(dve, r.s_hT_ps, t1, 2)
                        wait_reuse(dve, r.s_rows, t1, 2)
                        norm_apply(nc, dve, hn, xt(t1), t1, b1)
                    if exists(t0, NT):
                        norm_stats(nc, dve, m, qn, xt(t0), t0, b0)
                        norm_apply(nc, dve, qn, xt(t0), t0, b0)

                for op in (v.memset(kB[:, :, :, :, :, :], 0.0), v.memset(vB[:, :, :, :, :], 0.0)):
                    op.then_inc(s_init, 1)
                dve.wait_ge(s_init, 2)
                for par in range(2):
                    last = v.memset(vB[64 * par:64 * par + 64, :, :, :, 2 * HD + par:2 * HD + par + 1], 1.0)
                last.then_inc(s_init, 1)
                dve.wait_ge(s_init, 3)
                v.memset(r.cum[:, :], 0.0).then_inc(r.s_cum, 1)
                pipeline(dve, step, NT, 2, 1, 2)
                router_dve_tables(nc, dve, m, r)

            @block.sync
            def _(sp):
                def load(t, b):
                    wait_reuse(sp, s_v, t, 2)
                    sp.dma_start(ctxt[:, b, :], a["ctx"][bass.ds(t * P, P), :]).then_inc(s_ctx[b], 16)

                def step(u, j):
                    t, b, _u = tile_of(u, j, 1)
                    t2, b2, _u = tile_of(u, j, -2)
                    if exists(t, NT):
                        load(t, b)
                    if exists(t2, NT):
                        router_sp_keep(nc, sp, m, r, t2, b2)

                pipeline(sp, step, NT, 2, 1, 2)
                router_sp_tails(nc, sp, m, r)
                for b in range(2):
                    sp.wait_ge(r.s_kept[b], 16 * NT // 2)


class Shared:

    def __init__(self, nc, ctx, m, l):
        name = f"shared{l.n}"
        sem = lambda n: m.phase.take(f"{name}_{n}")
        self.l, self.chunks = l, len(l.shared)
        self.g_ps, self.u_ps, self.z_ps, self.cw_ps = m.bank[0:2], m.bank[2:4], m.bank[4:6], m.bank[6]
        self.act = ctx.enter_context(nc.sbuf_tensor(f"{name}_silu", [P, 2, 512], F32))
        self.hid = ctx.enter_context(nc.sbuf_tensor(f"{name}_hidden", [P, 2, self.chunks, 512], F32))
        self.s_gu, self.s_act, self.s_hid, self.s_z, self.s_x = sem("gate_up_ps"), sem("silu_done"), sem("hidden_done"), sem("out_ps"), sem("added")
        self.s_cw, self.s_cwT = sem("weights_ps"), sem("weights_sb")


BLOCK = 512
BLOCKS, BT = TOKENS // BLOCK, BLOCK // P


def shared_pe(nc, pe, m, s):
    mm, l = nc.tensor.matmul, s.l

    def down(blk):
        pe.wait_ge(s.s_hid, (blk + 1) * s.chunks)
        if l.bias:
            pe.wait_ge(s.s_cwT, blk + 1)
        for i in range(BT):
            t = blk * BT + i
            if t >= 2:
                pe.wait_ge(s.s_x, t - 1)
            z = s.z_ps[t % 2][:, 0:D]
            if l.bias:
                mm(z, m.cwT[:, t * P:(t + 1) * P], m.b2[:, :], start=True, stop=False)
            for c, (f0, fs) in enumerate(l.shared):
                last = mm(z, s.hid[0:fs, blk % 2, c, i * P:(i + 1) * P], m.sw_out[l.n][0:fs, c, :],
                          start=(c == 0 and not l.bias), stop=(c == s.chunks - 1))
            last.then_inc(s.s_z, 1)

    for blk in range(BLOCKS):
        cols = slice(blk * BLOCK, (blk + 1) * BLOCK)
        if l.bias:
            if blk:
                pe.wait_ge(s.s_cwT, blk)
            for i in range(BT):
                last = nc.tensor.transpose(s.cw_ps[0:17, i * P:(i + 1) * P], m.cw[:, blk * BT + i, :], m.ident[:, :])
            last.then_inc(s.s_cw, 1)
        for c, (f0, fs) in enumerate(l.shared):
            n = blk * s.chunks + c
            if n >= 2:
                pe.wait_ge(s.s_hid, n - 1)
            for half, bank in ((0, s.g_ps), (1, s.u_ps)):
                for d in range(DC):
                    last = mm(bank[n % 2][0:fs, :], m.sw_in[l.n][:, d, half * l.fs + f0:half * l.fs + f0 + fs], m.hT[:, d, cols],
                              start=(d == 0), stop=(d == DC - 1))
            last.then_inc(s.s_gu, 1)
        if blk:
            down(blk - 1)
    down(BLOCKS - 1)


def shared_act(nc, act, m, s):
    l = s.l
    for blk in range(BLOCKS):
        if l.bias:
            act.wait_ge(s.s_cw, blk + 1)
            nc.scalar.activation(m.cwT[:, blk * BLOCK:(blk + 1) * BLOCK], s.cw_ps[0:17, :], ACT.Copy).then_inc(s.s_cwT, 1)
        for c, (f0, fs) in enumerate(l.shared):
            n = blk * s.chunks + c
            act.wait_ge(s.s_gu, n + 1)
            if n >= 2:
                act.wait_ge(s.s_hid, n - 1)
            bias = m.sbias[0:fs, c, 0:1] if l.bias else 0.0
            nc.scalar.activation(s.act[0:fs, n % 2, :], s.g_ps[n % 2][0:fs, :], ACT.Silu, bias=bias).then_inc(s.s_act, 1)


def shared_dve(nc, dve, m, s):
    v, l = nc.vector, s.l

    def add(blk):
        for t in range(blk * BT, (blk + 1) * BT):
            dve.wait_ge(s.s_z, t + 1)
            v.tensor_tensor(m.x[:, t, :], s.z_ps[t % 2][:, 0:D], m.x[:, t, :], ALU.add).then_inc(s.s_x, 1)

    for blk in range(BLOCKS):
        for c, (f0, fs) in enumerate(l.shared):
            n = blk * s.chunks + c
            dve.wait_ge(s.s_act, n + 1)
            if blk >= 2:
                dve.wait_ge(s.s_z, (blk - 1) * BT)
            bias = m.sbias[0:fs, c, 1:2] if l.bias else 0.0
            v.scalar_tensor_tensor(s.hid[0:fs, blk % 2, c, :], s.u_ps[n % 2][0:fs, :], bias, s.act[0:fs, n % 2, :],
                                   ALU.add, ALU.mult).then_inc(s.s_hid, 1)
        if blk:
            add(blk - 1)
    add(BLOCKS - 1)


def shared_alone(nc, m, a, l):
    ctx = ExitStack()
    with ctx:
        m.cwT = ctx.enter_context(nc.sbuf_tensor("cwT", [17, TOKENS], F32))
        s = Shared(nc, ctx, m, l)
        with nc.Block() as block:

            @block.sync
            def _(sp):
                sp.dma_start(m.bias_in[:, :], a["b13"].rearrange("(o n) -> o n", o=1).to_broadcast([P, 16 * 352])).then_inc(m.sem_weights[0], 16)

            @block.tensor
            def _(pe):
                shared_pe(nc, pe, m, s)

            @block.scalar
            def _(act):
                shared_act(nc, act, m, s)

            @block.vector
            def _(dve):
                shared_dve(nc, dve, m, s)


def experts(nc, m, l):
    ctx = ExitStack()
    with ctx:
        def sb(name, shape, dt=F32):
            return ctx.enter_context(nc.sbuf_tensor(f"moe{l.n}_{name}", shape, dt))

        def sem(name):
            return m.phase.take(f"moe{l.n}_{name}")

        f, fc, kc, n = l.f, l.fchunk, l.f // l.fchunk, l.tiles
        xT_ps, gu_ps, hT_ps, y_ps = m.bank[0:2], m.bank[2:4], m.bank[4:6], m.bank[6:8]
        w_out = w_out_view(m, l)
        rows, y = sb("rows", [P, RING, ROW]), sb("y", [P, RING, D])
        xT, hT = sb("rowsT", [P, 2, DC, P]), sb("hiddenT", [fc, 2, kc, P])
        gu, sil, hid = sb("gate_up", [P, 2, 2 * f]), sb("silu", [P, 2, f]), sb("hidden", [P, 2, f])
        s_in, s_out = [sem(f"rows_in{i}") for i in range(RING)], [sem(f"rows_out{i}") for i in range(RING)]
        s_xT_ps, s_xT, s_gu_ps, s_gu = sem("rowsT_ps"), sem("rowsT_sb"), sem("gate_up_ps"), sem("gate_up_sb")
        s_sil, s_hid, s_hT_ps, s_hT, s_y_ps, s_y = sem("silu_done"), sem("hidden_done"), sem("hiddenT_ps"), sem("hiddenT_sb"), sem("y_ps"), sem("y_done")
        AHEAD = RING - 3

        with nc.Block() as block:

            @block.sync
            def _(sp):
                def load(u, j):
                    t, k, r = tile_of(u, j, 0, RING)
                    if not exists(t, n):
                        return
                    row = sp.value_load(m.tab[0:1, 1, bass.ds(t, 1)], min_val=0, max_val=l.zero_row)
                    if not isinstance(t, int) or t >= RING:
                        sp.wait_ge(s_out[k], r * 16)
                    sp.dma_start(rows[:, k, :], m.lists[l.n][bass.ds(row, P), :]).then_inc(s_in[k], 16)

                sp.wait_ge(m.sem_zero_lists, 32)
                pipeline(sp, load, n, RING, 0, 0)

            @block.tensor
            def _(pe):
                mm = nc.tensor.matmul

                def turn_rows(t, k, r):
                    pe.wait_ge(s_in[k], (r + 1) * 16)
                    wait_reuse(pe, s_xT, t, 2)
                    for c in range(DC):
                        last = nc.tensor.transpose(xT_ps[k % 2][:, c * P:(c + 1) * P], rows[:, k, c * P:(c + 1) * P], m.ident[:, :])
                    last.then_inc(s_xT_ps, 1)

                def gate_up(t, k):
                    e = pe.value_load(m.tab[0:1, 0, bass.ds(t, 1)], min_val=0, max_val=l.experts - 1)
                    pe.wait_ge(s_xT, t + 1)
                    wait_reuse(pe, s_hid, t, 2)
                    for c in range(DC):
                        last = mm(gu_ps[k % 2][:, 0:2 * f], xT[:, k % 2, c, :], m.w_in[:, c, bass.ds(e * (2 * f), 2 * f)], start=(c == 0), stop=(c == DC - 1))
                    last.then_inc(s_gu_ps, 1)

                def turn_hidden(t, k):
                    pe.wait_ge(s_hid, t + 1)
                    wait_reuse(pe, s_hT, t, 2)
                    for c in range(kc):
                        last = nc.tensor.transpose(hT_ps[k % 2][0:fc, c * P:(c + 1) * P], hid[:, k % 2, c * fc:(c + 1) * fc], m.ident[:, :])
                    last.then_inc(s_hT_ps, 1)

                def down(t, k):
                    e = pe.value_load(m.tab[0:1, 0, bass.ds(t, 1)], min_val=0, max_val=l.experts - 1)
                    pe.wait_ge(s_hT, t + 1)
                    wait_reuse(pe, s_y, t, 2)
                    for c in range(kc):
                        last = mm(y_ps[k % 2][:, 0:D], hT[:, k % 2, c, :], w_out[:, c, bass.ds(e * D, D)], start=(c == 0), stop=(c == kc - 1))
                    last.then_inc(s_y_ps, 1)

                def step(u, j):
                    t, k, _r = tile_of(u, j, 0, RING)
                    t1, k1, r1 = tile_of(u, j, 1, RING)
                    p1, q1, _r = tile_of(u, j, -1, RING)
                    p2, q2, _r = tile_of(u, j, -2, RING)
                    if exists(t, n):
                        gate_up(t, k)
                    if exists(p1, n):
                        turn_hidden(p1, q1)
                    if exists(t1, n):
                        turn_rows(t1, k1, r1)
                    if exists(p2, n):
                        down(p2, q2)

                pe.wait_ge(m.sem_weights[l.n], (6 if l.bias else 5) * 16)
                pipeline(pe, step, n, RING, 1, 2)

            @block.scalar
            def _(act):
                def keep_rowsT(t, k):
                    act.wait_ge(s_xT_ps, t + 1)
                    wait_reuse(act, s_gu_ps, t, 2)
                    nc.scalar.activation(xT[:, k % 2, :, :], xT_ps[k % 2][:, 0:D].rearrange("p (c n) -> p c n", c=DC), ACT.Copy).then_inc(s_xT, 1)

                def silu(t, k):
                    if l.bias:
                        act.wait_ge(s_gu, t + 1)
                        src = gu[:, k % 2, 0:f]
                    else:
                        act.wait_ge(s_gu_ps, t + 1)
                        src = gu_ps[k % 2][:, 0:f]
                    wait_reuse(act, s_hid, t, 2)
                    nc.scalar.activation(sil[:, k % 2, :], src, ACT.Silu).then_inc(s_sil, 1)

                def scale(t, k, r):
                    act.wait_ge(s_y_ps, t + 1)
                    if not isinstance(t, int) or t >= RING:
                        act.wait_ge(s_out[k], r * 16)
                    nc.scalar.activation(y[:, k, :], y_ps[k % 2][:, 0:D], ACT.Copy, scale=rows[:, k, WEIGHT:ROW]).then_inc(s_y, 1)

                def step(u, j):
                    t, k, _r = tile_of(u, j, 0, RING)
                    t1, k1, _r = tile_of(u, j, 1, RING)
                    p2, q2, r2 = tile_of(u, j, -2, RING)
                    if exists(t, n):
                        silu(t, k)
                    if exists(t1, n):
                        keep_rowsT(t1, k1)
                    if exists(p2, n) and l.bias:
                        scale(p2, q2, r2)

                pipeline(act, step, n, RING, 1, 2)

            @block.vector
            def _(dve):
                v = nc.vector

                def add_bias(t, k):
                    e = dve.value_load(m.tab[0:1, 0, bass.ds(t, 1)], min_val=0, max_val=l.experts - 1)
                    dve.wait_ge(s_gu_ps, t + 1)
                    wait_reuse(dve, s_hid, t, 2)
                    v.tensor_tensor(gu[:, k % 2, :], gu_ps[k % 2][:, 0:2 * f], m.bias_in[:, bass.ds(e * (2 * f), 2 * f)], ALU.add).then_inc(s_gu, 1)

                def hidden(t, k):
                    dve.wait_ge(s_sil, t + 1)
                    wait_reuse(dve, s_hT_ps, t, 2)
                    up = gu[:, k % 2, f:2 * f] if l.bias else gu_ps[k % 2][:, f:2 * f]
                    v.tensor_tensor(hid[:, k % 2, :], up, sil[:, k % 2, :], ALU.mult).then_inc(s_hid, 1)

                def keep_hiddenT(t, k):
                    dve.wait_ge(s_hT_ps, t + 1)
                    wait_reuse(dve, s_y_ps, t, 2)
                    v.tensor_copy(hT[:, k % 2, :, :], hT_ps[k % 2][0:fc, 0:kc * P].rearrange("p (c n) -> p c n", c=kc)).then_inc(s_hT, 1)

                def scale(t, k, r):
                    dve.wait_ge(s_y_ps, t + 1)
                    if not isinstance(t, int) or t >= RING:
                        dve.wait_ge(s_out[k], r * 16)
                    v.tensor_scalar(y[:, k, :], y_ps[k % 2][:, 0:D], rows[:, k, WEIGHT:ROW], None, ALU.mult).then_inc(s_y, 1)

                def step(u, j):
                    t, k, _r = tile_of(u, j, 0, RING)
                    p1, q1, _r = tile_of(u, j, -1, RING)
                    p2, q2, r2 = tile_of(u, j, -2, RING)
                    if exists(t, n) and l.bias:
                        add_bias(t, k)
                    if exists(p1, n):
                        keep_hiddenT(p1, q1)
                    if exists(t, n):
                        hidden(t, k)
                    if exists(p2, n) and not l.bias:
                        scale(p2, q2, r2)

                if l.bias:
                    dve.wait_ge(m.sem_weights[l.n], 6 * 16)
                pipeline(dve, step, n, RING, 0, 2)

            @block.gpsimd
            def _(pool):
                def send(u, j):
                    t, k, _r = tile_of(u, j, 0, RING)
                    if not exists(t, n):
                        return
                    pool.wait_ge(s_y, t + 1)
                    hold(pool, m)
                    pool.indirect_dma_start(m.res[l.n][:, :], bass.IndirectOffsetOnAxis(ap=rows[:, k, DEST:DEST + 1].bitcast(U32), axis=0),
                                            y[:, k, :], None, bounds_check=l.out_rows - 1, oob_is_err=False).then_inc(s_out[k], 16)

                pipeline(pool, send, n, RING, 0, 0)
                for k in range(RING):
                    pool.wait_ge(s_out[k], 16 * (n // RING))


def attend_masked(nc, m, a):
    l0, l = LAYERS
    ctx = ExitStack()
    with ctx:
        def sb(name, shape, dt=F32):
            return ctx.enter_context(nc.sbuf_tensor("masked_" + name, shape, dt))

        def sem(name):
            return m.phase.take("masked_" + name)

        qT_ps, kT_ps, s_ps, pT_ps, o_ps, h_ps = m.bank[0], m.bank[1], m.bank[2], m.bank[3], m.bank[4], m.bank[7]
        qn, hn = Norm(nc, ctx, m, "norm_m"), Norm(nc, ctx, m, "norm_g")
        r = Router(nc, ctx, m, l, h_ps)
        sh = Shared(nc, ctx, m, l)
        res = sb("results", [P, 2, l0.top * D])
        qT, kT, pT = sb("qT", [P, 2, D]), sb("kT", [P, 2, D]), sb("probsT", [P, 2, P])
        sm, pr = sb("scores", [P, 2, S]), sb("probs", [P, 2, P])
        negmax, sums, rec = sb("neg_row_max", [P, 2, 1]), sb("row_sum", [P, 2, 1]), sb("recip", [P, 2, 1])
        keep, fill, valid = sb("keep", [P, NT, S]), sb("fill", [P, NT, S]), sb("valid", [P, NT])
        ctxt, val = sb("context", [P, 2, D]), sb("values", [P, 2, D])
        s_ctx, s_val = [sem("context_even"), sem("context_odd")], [sem("values_even"), sem("values_odd")]
        s_init, s_mask = sem("zeroed"), sem("mask_steps")
        s_res = [sem("results_even"), sem("results_odd")]
        s_add, s_sum = sem("first_added"), sem("all_added")
        s_qT, s_qT_sb, s_kT_sb, s_sc, s_sm, s_filled, s_max, s_exp = (
            sem("qT_ps"), sem("qT_sb"), sem("kT_sb"), sem("scores_ps"), sem("scores_sb"), sem("scores_filled"), sem("row_max"), sem("probs_done"))
        s_rec, s_valid, s_pT, s_pT_sb, s_o, s_x = sem("recip_done"), sem("scale_done"), sem("probsT_ps"), sem("probsT_sb"), sem("out_ps"), sem("x_done")

        with nc.Block() as block:

            @block.sync
            def _(sp):
                def load_results(t, b):
                    wait_reuse(sp, s_sum, t, 2)
                    sp.dma_start(res[:, b, :], m.res[0][bass.ds(t * (P * l0.top), P * l0.top), :].rearrange("(p k) d -> p (k d)", k=l0.top)).then_inc(s_res[b], 16)

                def load_context(t, b):
                    wait_reuse(sp, s_qT, t, 2)
                    sp.dma_start(ctxt[:, b, :], a["ctx"][bass.ds(t * P, P), :]).then_inc(s_ctx[b], 16)

                def load_values(t, b):
                    wait_reuse(sp, s_o, t, 2)
                    sp.dma_start(val[:, b, :], a["ctx"][bass.ds(t * P, P), :]).then_inc(s_val[b], 16)

                def step(u, j):
                    t0, b0, _u = tile_of(u, j, 2)
                    t, b, _u = tile_of(u, j, 1)
                    t1, b1, _u = tile_of(u, j, 0)
                    t2, b2, _u = tile_of(u, j, -2)
                    if exists(t0, NT):
                        load_results(t0, b0)
                    if exists(t, NT):
                        load_context(t, b)
                    if exists(t1, NT):
                        load_values(t1, b1)
                    if exists(t2, NT):
                        router_sp_keep(nc, sp, m, r, t2, b2)

                pipeline(sp, step, NT, 2, 2, 2)
                router_sp_tails(nc, sp, m, r)
                for b in range(2):
                    sp.wait_ge(r.s_kept[b], 16 * NT // 2)

            @block.tensor
            def _(pe):
                mm = nc.tensor.matmul

                def turn(t, b, u):
                    pe.wait_ge(s_ctx[b], u * 16 + 16)
                    pe.wait_ge(qn.s_out, t + 1)
                    wait_reuse(pe, s_qT_sb, t, 1)
                    wait_reuse(pe, s_kT_sb, t, 1)
                    for c in range(DC):
                        nc.tensor.transpose(qT_ps[:, c * P:(c + 1) * P], qn.out[:, b, c * P:(c + 1) * P], m.ident[:, :])
                        last = nc.tensor.transpose(kT_ps[:, c * P:(c + 1) * P], ctxt[:, b, c * P:(c + 1) * P], m.ident[:, :])
                    last.then_inc(s_qT, 1)

                def scores(t, b):
                    pe.wait_ge(s_qT_sb, t + 1)
                    pe.wait_ge(s_kT_sb, t + 1)
                    wait_reuse(pe, s_sm, t, 1)
                    for batch in range(2):
                        rows = slice(64 * batch, 64 * batch + 64)
                        for c in range(DC):
                            cols = slice(c * P + 64 * batch, c * P + 64 * batch + 64)
                            last = mm(s_ps[rows, 0:S], qT[:, b, cols], kT[:, b, cols], start=(c == 0), stop=(c == DC - 1))
                    last.then_inc(s_sc, 1)

                def turn_probs(t, b):
                    pe.wait_ge(s_exp, t + 1)
                    wait_reuse(pe, s_pT_sb, t, 1)
                    nc.tensor.transpose(pT_ps[:, 0:P], pr[:, b, :], m.ident[:, :]).then_inc(s_pT, 1)

                def attend(t, b, u):
                    pe.wait_ge(s_val[b], u * 16 + 16)
                    pe.wait_ge(s_pT_sb, t + 1)
                    wait_reuse(pe, s_x, t, 1)
                    mm(o_ps[:, 0:D], pT[:, b, :], val[:, b, :], start=True, stop=True).then_inc(s_o, 1)

                def step(u, j):
                    t, b, u0 = tile_of(u, j, 0)
                    t1, b1, u1 = tile_of(u, j, -1)
                    t2, b2, _u = tile_of(u, j, -2)
                    if exists(t, NT):
                        turn(t, b, u0)
                    if exists(t1, NT):
                        turn_probs(t1, b1)
                    if exists(t2, NT):
                        router_pe_transpose(nc, pe, m, r, hn.out, hn.s_out, t2, b2)
                    if exists(t, NT):
                        scores(t, b)
                    if exists(t1, NT):
                        attend(t1, b1, u1)
                    if exists(t2, NT):
                        router_pe_logits(nc, pe, m, r, t2, b2)
                        router_pe_rank(nc, pe, m, r, t2, b2)

                pe.wait_ge(s_init, 1)
                pipeline(pe, step, NT, 2, 0, 2)
                pe.wait_ge(s_x, NT)
                router_pe_tables(nc, pe, m, r)
                for b in range(2):
                    pe.wait_ge(r.s_kept[b], 16 * NT // 2)
                shared_pe(nc, pe, m, sh)

            @block.scalar
            def _(act):
                copy = lambda o, i: nc.scalar.activation(o, i, ACT.Copy)

                def keep_qT(t, b):
                    act.wait_ge(s_qT, t + 1)
                    wait_reuse(act, s_sc, t, 2)
                    copy(qT[:, b, :], qT_ps[:, 0:D]).then_inc(s_qT_sb, 1)

                def exps(t, b):
                    act.wait_ge(s_max, t + 1)
                    wait_reuse(act, s_pT, t, 2)
                    wait_reuse(act, s_valid, t, 2)
                    for batch in range(2):
                        rows = slice(64 * batch, 64 * batch + 64)
                        last = nc.scalar.activation(pr[rows, b, 64 * batch:64 * batch + 64], sm[rows, b, :], ACT.Exp,
                                                    bias=negmax[rows, b, :], accum_out=sums[rows, b, :])
                    last.then_inc(s_exp, 1)

                def keep_pT(t, b):
                    act.wait_ge(s_pT, t + 1)
                    wait_reuse(act, s_o, t, 2)
                    copy(pT[:, b, :], pT_ps[:, 0:P]).then_inc(s_pT_sb, 1)

                def step(u, j):
                    t, b, _u = tile_of(u, j, 0)
                    t1, b1, _u = tile_of(u, j, -1)
                    t2, b2, u2 = tile_of(u, j, -2)
                    if exists(t, NT):
                        keep_qT(t, b)
                    if exists(t1, NT):
                        keep_pT(t1, b1)
                    if exists(t2, NT):
                        router_act_hT(nc, act, m, r, t2, b2, u2)
                    if exists(t, NT):
                        exps(t, b)
                    if exists(t2, NT):
                        router_act_exps(nc, act, m, r, t2, b2)
                        router_act_rows(nc, act, m, r, hn.out, t2, b2, u2)

                load_experts(act, m, a, l)
                act.wait_ge(s_init, 1)
                pipeline(act, step, NT, 2, 0, 2)
                shared_act(nc, act, m, sh)

            @block.gpsimd
            def _(pool):
                def step(u, j):
                    t, b, _u = tile_of(u, j, 1)
                    t1, b1, _u = tile_of(u, j, -1)
                    t2, b2, _u = tile_of(u, j, -2)
                    if exists(t1, NT):
                        norm_rstd(nc, pool, m, hn, t1, b1)
                    if exists(t, NT):
                        norm_rstd(nc, pool, m, qn, t, b)
                    if exists(t2, NT):
                        router_pool_send(nc, pool, m, r, t2, b2)

                pipeline(pool, step, NT, 2, 1, 2)
                for b in range(2):
                    pool.wait_ge(r.s_sent[b], 16 * l.top * NT // 2)

            @block.vector
            def _(dve):
                v = nc.vector

                def xt(t):
                    return m.x[:, bass.ds(t, 1), :].rearrange("p o n -> p (o n)")

                def add_results(t, b, u):
                    dve.wait_ge(s_res[b], u * 16 + 16)
                    v.tensor_tensor(xt(t), xt(t), res[:, b, 0:D], ALU.add).then_inc(s_add, 1)
                    dve.wait_ge(s_add, t + 1)
                    v.tensor_tensor(xt(t), xt(t), res[:, b, D:2 * D], ALU.add).then_inc(s_sum, 1)
                    dve.wait_ge(s_sum, t + 1)

                def keep_kT(t, b):
                    dve.wait_ge(s_qT, t + 1)
                    wait_reuse(dve, s_sc, t, 2)
                    v.tensor_copy(kT[:, b, :], kT_ps[:, 0:D]).then_inc(s_kT_sb, 1)

                def mask_scores(t, b):
                    dve.wait_ge(s_sc, t + 1)
                    wait_reuse(dve, s_exp, t, 2)
                    v.scalar_tensor_tensor(sm[:, b, :], s_ps[:, 0:S], float(D) ** -0.5, keep[:, bass.ds(t, 1), :].rearrange("p o s -> p (o s)"),
                                           ALU.mult, ALU.mult).then_inc(s_sm, 1)
                    dve.wait_ge(s_sm, t + 1)
                    v.tensor_tensor(sm[:, b, :], sm[:, b, :], fill[:, bass.ds(t, 1), :].rearrange("p o s -> p (o s)"), ALU.add).then_inc(s_filled, 1)
                    dve.wait_ge(s_filled, t + 1)
                    v.tensor_reduce(negmax[:, b, :], sm[:, b, :], AX_X, ALU.max, negate=True).then_inc(s_max, 1)

                def residual(t, b):
                    dve.wait_ge(s_exp, t + 1)
                    v.reciprocal(rec[:, b, :], sums[:, b, :]).then_inc(s_rec, 1)
                    dve.wait_ge(s_rec, t + 1)
                    v.tensor_tensor(rec[:, b, :], rec[:, b, :], valid[:, bass.ds(t, 1)], ALU.mult).then_inc(s_valid, 1)
                    dve.wait_ge(s_valid, t + 1)
                    dve.wait_ge(s_o, t + 1)
                    v.scalar_tensor_tensor(xt(t), o_ps[:, 0:D], rec[:, b, :], xt(t), ALU.mult, ALU.add).then_inc(s_x, 1)
                    dve.wait_ge(s_x, t + 1)
                    norm_stats(nc, dve, m, hn, xt(t), t, b)

                def step(u, j):
                    t0, b0, u0 = tile_of(u, j, 1)
                    t, b, _u = tile_of(u, j, 0)
                    t1, b1, _u = tile_of(u, j, -1)
                    t2, b2, u2 = tile_of(u, j, -2)
                    if exists(t, NT):
                        keep_kT(t, b)
                        mask_scores(t, b)
                    if exists(t2, NT):
                        router_dve_choose(nc, dve, m, r, t2, b2)
                    if exists(t1, NT):
                        residual(t1, b1)
                    if exists(t0, NT):
                        add_results(t0, b0, u0)
                        norm_stats(nc, dve, m, qn, xt(t0), t0, b0)
                    if exists(t2, NT):
                        router_dve_place(nc, dve, m, r, t2, b2, u2)
                    if exists(t1, NT):
                        wait_reuse(dve, r.s_hT_ps, t1, 2)
                        wait_reuse(dve, r.s_rows, t1, 2)
                        norm_apply(nc, dve, hn, xt(t1), t1, b1)
                    if exists(t0, NT):
                        wait_reuse(dve, s_qT, t0, 2)
                        norm_apply(nc, dve, qn, xt(t0), t0, b0)

                v.memset(pr[:, :, :], 0.0).then_inc(s_init, 1)
                v.tensor_scalar(keep[:, :, :], m.mask8[:, :, :], 1.0, None, ALU.mult).then_inc(s_mask, 1)
                dve.wait_ge(s_mask, 1)
                v.tensor_scalar(fill[:, :, :], keep[:, :, :], -1.0, 1e30, ALU.add, ALU.mult)
                v.tensor_reduce(valid[:, :], keep[:, :, :], AX_X, ALU.max).then_inc(s_mask, 1)
                dve.wait_ge(s_mask, 2)
                v.memset(r.cum[:, :], 0.0).then_inc(r.s_cum, 1)
                pipeline(dve, step, NT, 2, 1, 2)
                router_dve_tables(nc, dve, m, r)
                shared_dve(nc, dve, m, sh)


def finish(nc, m, out):
    l = LAYERS[1]
    ctx = ExitStack()
    with ctx:
        def sem(name):
            return m.phase.take("finish_" + name)

        res = ctx.enter_context(nc.sbuf_tensor("finish_results", [P, 2, l.top * D], F32))
        part = ctx.enter_context(nc.sbuf_tensor("finish_sums", [P, 2, 3 * D], F32))
        s_res = [sem("results_even"), sem("results_odd")]
        s_a, s_b, s_c, s_d = sem("six_to_three"), sem("three_to_two"), sem("two_to_one"), sem("summed")
        s_out = sem("stored")
        with nc.Block() as block:

            @block.sync
            def _(sp):
                def load(u, j):
                    t, b, _u = tile_of(u, j, 0)
                    if not exists(t, NT):
                        return
                    wait_reuse(sp, s_a, t, 2)
                    sp.dma_start(res[:, b, :], m.res[1][bass.ds(t * (P * l.top), P * l.top), :].rearrange("(p k) d -> p (k d)", k=l.top)).then_inc(s_res[b], 16)

                pipeline(sp, load, NT, 2, 0, 0)

            @block.vector
            def _(dve):
                v = nc.vector

                def step(u, j):
                    t, b, r = tile_of(u, j, 0)
                    if not exists(t, NT):
                        return
                    xt = m.x[:, bass.ds(t, 1), :].rearrange("p o n -> p (o n)")
                    dve.wait_ge(s_res[b], r * 16 + 16)
                    v.tensor_tensor(part[:, b, :], res[:, b, 0:3 * D], res[:, b, 3 * D:6 * D], ALU.add).then_inc(s_a, 1)
                    dve.wait_ge(s_a, t + 1)
                    v.tensor_tensor(xt, xt, part[:, b, 0:D], ALU.add).then_inc(s_b, 1)
                    v.tensor_tensor(part[:, b, D:2 * D], part[:, b, D:2 * D], part[:, b, 2 * D:3 * D], ALU.add).then_inc(s_c, 1)
                    dve.wait_ge(s_b, t + 1)
                    dve.wait_ge(s_c, t + 1)
                    v.tensor_tensor(xt, xt, part[:, b, D:2 * D], ALU.add).then_inc(s_d, 1)

                pipeline(dve, step, NT, 2, 0, 0)

            @block.scalar
            def _(act):
                with act.Fori(0, NT) as t:
                    act.wait_ge(s_d, t + 1)
                    act.dma_start(out.rearrange("(t p) d -> p t d", p=P)[:, bass.ds(t, 1), :], m.x[:, bass.ds(t, 1), :]).then_inc(s_out, 16)
                act.wait_ge(s_out, 16 * NT)


def kernel(**inputs):
    import numpy as np
    import concourse.bacc as bacc
    from concourse.bass_utils import run_bass_kernel_spmd as run

    i = {k: np.asarray(v) for k, v in inputs.items()}
    lay = np.ascontiguousarray
    arrays = {
        "x": lay(i["x"].reshape(TOKENS, D)),
        "ctx": lay(i["ctx_2048"].reshape(TOKENS, D)),
        "mask": lay(i["mask_BxS2_bk0"]),
        "wqT": lay(i["L0_xattn_W_q"].T), "wkT": lay(i["L0_xattn_W_k"].T),
        "wvT": lay(i["L0_xattn_W_v"].T), "woT": lay(i["L0_xattn_W_o"].T),
        "gate0": lay(i["L0_ffn_gate_w"].T),
        "w13": lay(np.concatenate([i["L0_ffn_w1"], i["L0_ffn_w3"]], 1).transpose(2, 0, 1).reshape(D, -1)),
        "b13": lay(np.concatenate([i["L0_ffn_b1"], i["L0_ffn_b3"]], 1).reshape(-1)),
        "w2": lay(i["L0_ffn_w2"].transpose(2, 0, 1).reshape(176, -1)),
        "b2aug": lay(np.concatenate([i["L0_ffn_b2"], i["L0_ffn_sb2"][None]], 0)),
        "sw13": lay(np.concatenate([i["L0_ffn_sw1"], i["L0_ffn_sw3"]], 0).T),
        "sb1": lay(i["L0_ffn_sb1"]), "sb3": lay(i["L0_ffn_sb3"]),
        "sw2": lay(i["L0_ffn_sw2"].T),
        "gate1": lay(i["L1_ffn_gate_w"]),
        "wgu": lay(np.concatenate([i["L1_ffn_wg"], i["L1_ffn_wu"]], 2).transpose(1, 0, 2).reshape(D, -1)),
        "wd": lay(i["L1_ffn_wd"].transpose(1, 0, 2).reshape(96, -1)),
        "sgu": lay(np.concatenate([i["L1_ffn_sg"], i["L1_ffn_su"]], 1)),
        "sd": lay(i["L1_ffn_sd"]),
    }
    nc = bacc.Bacc("TRN2", target_bir_lowering=False, num_devices=1)
    a = {k: nc.dram_tensor(f"in_{k}", v.shape, mybir.dt.from_np(v.dtype), kind="ExternalInput").ap()
         for k, v in arrays.items()}
    out = nc.dram_tensor("out_x", (TOKENS, D), F32, kind="ExternalOutput").ap()
    program(nc, a, out)
    r = run(nc, [{f"in_{k}": v for k, v in arrays.items()}], core_ids=[0])
    return r.results[0]["out_x"].reshape(B, S, D)
```

```python
import concourse.bass as bass
from concourse import mybir
from contextlib import ExitStack

F32 = mybir.dt.float32
BF16 = mybir.dt.bfloat16
U32 = mybir.dt.uint32
I32 = mybir.dt.int32
U8 = mybir.dt.uint8
ALU = mybir.AluOpType
ACT = mybir.ActivationFunctionType
AX_X = mybir.AxisListType.X

P = 128
B, S, D = 32, 64, 256
TOKENS = B * S
NT = TOKENS // P
DC = D // P
HEADS, HD = 8, 32
HC = HEADS // DC
EPS = 1e-5
DEST = D
WEIGHT = D + 1
ROW = D + 2
LIST = TOKENS + P
RING = 8
TAB_PAD = 8

class Layer:

    def __init__(self, n, experts, top, f, fchunk, bias, shared, fs):
        self.n, self.experts, self.top, self.f, self.fchunk = n, experts, top, f, fchunk
        self.bias = bias
        self.shared, self.fs = shared, fs
        self.tiles = TOKENS * top // P + experts
        self.zero_row = experts * LIST
        self.list_rows = self.zero_row + P
        self.out_rows = TOKENS * top


LAYERS = [
    Layer(n=0, experts=16, top=2, f=176, fchunk=88, bias=True, shared=[(0, 128), (128, 128), (256, 96)], fs=352),
    Layer(n=1, experts=32, top=6, f=96, fchunk=96, bias=False, shared=[(0, 96), (96, 96)], fs=192),
]


class Memory:
    pass


def exists(tile, count):
    return not isinstance(tile, int) or 0 <= tile < count


def wait_reuse(eng, sem, tile, lag, each=1):
    if not isinstance(tile, int) or tile - lag >= 0:
        eng.wait_ge(sem, (tile - lag + 1) * each)


def hold(eng, m):
    eng.sem_inc(m.s_held, 1)


def pipeline(eng, step, tiles, unroll, lead, lag, load=None):
    first = unroll + lag
    rounds = (tiles - lead - first) // unroll

    def peeled(start, stop):
        for i0 in range(start, stop, unroll):
            count = min(unroll, stop - i0)
            values = load(i0, count) if load else None
            for i in range(i0, i0 + count):
                step(i // unroll, i % unroll, *([values[i - i0:]] if load else []))

    peeled(-lead, first)
    with eng.Fori(1, 1 + rounds) as u:
        values = load(u * unroll + lag, unroll) if load else None
        for j in range(unroll):
            step(u, j + lag, *([values[j:]] if load else []))
    peeled(first + rounds * unroll, tiles + lag)


def table_values(nc, m, engine, row, first, count, most):
    at = first + TAB_PAD
    return nc.values_load_multi_w_load_instructions(
        m.tab[0:1, row, bass.ds(at, count)], engines=[engine], min_val=0, max_val=most,
        skip_runtime_bounds_check_because="the tables' entries are clamped where they are made, and zero beside them")[1]


def shifted(u, j, by, unroll):
    return u + (j + by) // unroll, (j + by) % unroll


class Phase:

    def __init__(self, nc):
        self.nc, self.taken = nc, []

    def take(self, name):
        self.taken.append(self.nc.alloc_semaphore(name))
        return self.taken[-1]

    def end(self):
        self.nc.clear_and_free_semaphores(self.taken)
        self.nc.all_engine_barrier()
        self.taken = []


def program(nc, a, out):
    ctx = ExitStack()
    with ctx:
        def sb(name, shape, dt=F32):
            return ctx.enter_context(nc.sbuf_tensor(name, shape, dt))

        def sem(name):
            return nc.alloc_semaphore(name)

        m = Memory()
        m.phase = Phase(nc)
        m.x = sb("x_all", [P, NT, D])
        m.hT = sb("hT_all", [P, DC, TOKENS])
        m.w_in = sb("w_in", [P, DC, 32 * 192])
        m.w_out = sb("w_out", [96, 32 * D])
        m.wq = sb("wq", [P, P])
        m.wk = sb("wk", [P, P])
        m.wv = sb("wv", [P, 2, P])
        m.wo = sb("wo", [P, P])
        m.gate = [sb("gate0", [P, DC, 16]), sb("gate1", [P, DC, 32])]
        m.sw_in = [sb("sw_in0", [P, DC, 704]), sb("sw_in1", [P, DC, 384])]
        m.sw_out = [sb("sw_out0", [P, 3, D]), sb("sw_out1", [96, 2, D])]
        m.sbias = sb("sbias", [P, 3, 2])
        m.b2 = sb("b2", [17, D])
        m.mask8 = sb("mask8", [P, NT, S], U8)
        m.ident = sb("ident", [P, P])
        m.upper = sb("upper", [P, P], BF16)
        m.ones = sb("ones", [P, P], BF16)
        m.iota_p = sb("iota_p", [P, 1])
        m.mhalf = sb("mhalf", [P, 2])
        m.iota_e = [sb("iota_e0", [P, 2, 16]), sb("iota_e1", [P, 6, 32])]
        m.list0 = [sb("list0_0", [P, 16]), sb("list0_1", [P, 32])]
        m.dest = [sb("dest0", [P, NT, 2], I32), sb("dest1", [P, NT, 6], I32)]
        m.zrow = [sb("zrow0", [P, ROW]), sb("zrow1", [P, ROW])]
        m.tab = sb("tab", [1, 3, P + 2 * TAB_PAD], I32)
        m.cw = sb("cw", [P, NT, 17])
        m.bank = [ctx.enter_context(nc.psum_tensor(f"bank{i}", [P, 512], F32)) for i in range(8)]
        m.lists = [nc.dram_tensor(f"lists{l.n}", (l.list_rows, ROW), F32, kind="Internal").ap() for l in LAYERS]
        m.res = [nc.dram_tensor(f"results{l.n}", (l.out_rows, D), F32, kind="Internal").ap() for l in LAYERS]

        m.sem_weights = [sem("loaded_moe0"), sem("loaded_moe1")]
        m.sem_small = sem("loaded_small")
        m.s_held = sem("waits_ended")
        m.sem_zero_lists = sem("zero_lists")

        setup(nc, m, a)
        m.phase.end()
        attend_heads(nc, m, a)
        m.phase.end()
        with nc.sbuf_tensor("bias_in", [P, 16 * 352], F32) as m.bias_in:
            shared_alone(nc, m, a, LAYERS[0])
            m.phase.end()
            experts(nc, m, LAYERS[0])
            m.phase.end()
        attend_masked(nc, m, a)
        m.phase.end()
        experts(nc, m, LAYERS[1])
        m.phase.end()
        finish(nc, m, out)


def load_experts(eng, m, a, l):
    s = m.sem_weights[l.n]
    w_in, w_out = (a["w13"], a["w2"]) if l.n == 0 else (a["wgu"], a["wd"])
    n = l.experts * 2 * l.f
    quarter = n // 4
    for q in range(4):
        eng.dma_start(m.w_in[:, :, q * quarter:(q + 1) * quarter],
                      w_in.rearrange("(c p) n -> p c n", p=P)[:, :, q * quarter:(q + 1) * quarter]).then_inc(s, 16)
    eng.dma_start(w_out_view(m, l), w_out.rearrange("(c p) n -> p c n", p=l.fchunk)).then_inc(s, 16)


def w_out_view(m, l):
    return m.w_out[0:l.fchunk, :].rearrange("p (c n) -> p c n", c=l.f // l.fchunk)


def setup(nc, m, a):
    ctx = ExitStack()
    with ctx:
        def sem(name):
            return m.phase.take(name)
        s_x, s_att = sem("loaded_x"), sem("loaded_attention")
        s_zero, s_made = sem("zeroed"), sem("constants_made")
        s_zrow = sem("zero_rows_made")
        it = ctx.enter_context(nc.sbuf_tensor("iota_tmp", [P, 6 * 32 + 1], I32))
        with nc.Block() as block:

            @block.sync
            def _(sp):
                sp.wait_ge(s_zero, 1)
                for half in range(2):
                    r = slice(64 * half, 64 * half + 64)
                    for w, src in ((m.wq, a["wqT"]), (m.wk, a["wkT"]), (m.wo, a["woT"])):
                        sp.dma_start(w[r, r], src).then_inc(s_att, 16)
                    for dup in range(2):
                        sp.dma_start(m.wv[r, half, 64 * dup:64 * dup + 64], a["wvT"]).then_inc(s_att, 16)
                for q in range(4):
                    t = slice(4 * q, 4 * q + 4)
                    sp.dma_start(m.x[:, t, :], a["x"].rearrange("(t p) d -> p t d", p=P)[:, t, :]).then_inc(s_x, 16)
                sp.wait_ge(s_att, 10 * 16)
                sp.wait_ge(s_x, 4 * 16)

            @block.scalar
            def _(act):
                small = [(m.gate[n][:, :, :], g.rearrange("(c p) e -> p c e", p=P)) for n, g in ((0, a["gate0"]), (1, a["gate1"]))]
                small += [(m.b2[:, :], a["b2aug"])]
                small += [(m.sbias[0:fs, c, k:k + 1], b.rearrange("(f o) -> f o", o=1)[f0:f0 + fs, :]) for c, (f0, fs) in enumerate(LAYERS[0].shared)
                          for k, b in ((0, a["sb1"]), (1, a["sb3"]))]
                small += [(m.sw_in[n][:, :, :], w.rearrange("(c p) n -> p c n", p=P)) for n, w in ((0, a["sw13"]), (1, a["sgu"]))]
                small += [(m.sw_out[0][0:fs, c, :], a["sw2"][f0:f0 + fs, :]) for c, (f0, fs) in enumerate(LAYERS[0].shared)]
                small += [(m.sw_out[1][:, :, :], a["sd"].rearrange("(c p) n -> p c n", p=96))]
                small += [(m.mask8[64 * h:64 * h + 64, :, :],
                           a["mask"].rearrange("(t h) s -> h t s", h=2)[h:h + 1, :, :].to_broadcast([64, NT, S])) for h in range(2)]
                m.small_count = 16 * len(small)
                for dst, src in small:
                    act.dma_start(dst, src).then_inc(m.sem_small, 16)
                act.wait_ge(s_zrow, 4)
                for l in LAYERS:
                    act.dma_start(m.lists[l.n][l.zero_row:l.zero_row + P, :], m.zrow[l.n][:, :]).then_inc(m.sem_zero_lists, 16)
                load_experts(act, m, a, LAYERS[0])
                act.wait_ge(m.sem_small, m.small_count)

            @block.gpsimd
            def _(pool):
                g = nc.gpsimd
                made = [0]

                def then(op):
                    made[0] += 1
                    op.then_inc(s_made, 1)
                    pool.wait_ge(s_made, made[0])

                for l in LAYERS:
                    g.iota(m.zrow[l.n][:, DEST:DEST + 1].bitcast(I32), pattern=[[1, 1]], base=l.out_rows,
                           channel_multiplier=1).then_inc(s_zrow, 1)
                g.memset(m.mhalf[:, :], -0.5)
                g.memset(m.ident[:, :], 0.0)
                g.memset(m.ones[:, :], 1.0)
                then(g.memset(m.upper[:, :], 1.0))
                g.affine_select(out=m.ident[:, :], in_=m.ident[:, :], compare_op=ALU.not_equal, fill=1.0,
                                base=0, pattern=[[-1, P]], channel_multiplier=1)
                g.affine_select(out=m.upper[:, :], in_=m.upper[:, :], compare_op=ALU.is_gt, fill=0.0,
                                base=0, pattern=[[1, P]], channel_multiplier=-1)
                then(g.iota(it[:, 192:193], pattern=[[1, 1]], base=0, channel_multiplier=1))
                then(g.tensor_copy(m.iota_p[:, :], it[:, 192:193]))
                for l in LAYERS:
                    k, e = l.top, l.experts
                    g.iota(m.dest[l.n][:, :, :], pattern=[[P * k, NT], [1, k]], base=0, channel_multiplier=k)
                    numbers = it[:, 0:k * e].rearrange("p (k e) -> p k e", k=k)
                    then(g.iota(numbers, pattern=[[0, k], [1, e]], base=0, channel_multiplier=0))
                    g.tensor_copy(m.iota_e[l.n][:, :, :], numbers)
                    then(g.tensor_scalar(m.list0[l.n][:, :], numbers[:, 0, :], float(LIST), 0.0, ALU.mult, ALU.add))

            @block.vector
            def _(dve):
                v = nc.vector
                for w in (m.wq[:, :], m.wk[:, :], m.wo[:, :]):
                    v.memset(w, 0.0)
                v.memset(m.wv[:, :, :], 0.0)
                for l in LAYERS:
                    v.memset(m.zrow[l.n][:, 0:D], 0.0)
                    v.memset(m.zrow[l.n][:, WEIGHT:ROW], 0.0).then_inc(s_zrow, 1)
                v.memset(m.tab[:, :, :], 0)
                v.memset(m.cw[:, :, 16:17], 1.0).then_inc(s_zero, 1)


Q, H = 0, 1


class Norms:

    def __init__(self, nc, ctx, m, name, h_lag):
        sb = lambda n, shape: ctx.enter_context(nc.sbuf_tensor(f"{name}_{n}", [P, 2] + shape, F32))
        sem = lambda n: m.phase.take(f"{name}_{n}")
        self.h_lag = h_lag
        self.stats, self.mv = sb("stats", [2, 6]), sb("mean_var", [2, 2])
        self.var, self.rstd, self.shift = sb("var_eps", [2]), sb("rstd", [2]), sb("shift", [2])
        self.out = [sb("queries", [D]), sb("input", [D])]
        self.s_stats, self.s_mv = [sem("stats_q"), sem("stats_h")], [sem("mean_var_q"), sem("mean_var_h")]
        self.s_var, self.s_rstd, self.s_shift = sem("var_eps_done"), sem("rstd_done"), sem("shift_done")
        self.s_out = [sem("normed_q"), sem("normed_h")]

    def tile(self, u, j, side):
        return tile_of(u, j, 1 if side == Q else -self.h_lag)[0:2]

    def sides(self, u, j):
        return [side for side in (Q, H) if exists(self.tile(u, j, side)[0], NT)]


def norm_stats(nc, dve, m, n, u, j, side, x):
    t, b = n.tile(u, j, side)
    hold(dve, m)
    nc.vector.bn_stats(n.stats[:, j % 2, side, :], x).then_inc(n.s_stats[side], 1)
    dve.wait_ge(n.s_stats[side], t + 1)
    hold(dve, m)
    nc.vector.bn_aggr(n.mv[:, j % 2, side, :], n.stats[:, j % 2, side, :]).then_inc(n.s_mv[side], 1)


def norm_var(nc, dve, m, n, u, j):
    for side in n.sides(u, j):
        dve.wait_ge(n.s_mv[side], n.tile(u, j, side)[0] + 1)
    if n.sides(u, j):
        nc.vector.tensor_scalar(n.var[:, j % 2, :], n.mv[:, j % 2, :, 1], EPS, None, ALU.add).then_inc(n.s_var, 1)


def norm_rstd(nc, pool, m, n, u, j):
    i = u * 2 + j
    if not n.sides(u, j):
        return
    for side in n.sides(u, j):
        wait_reuse(pool, n.s_out[side], n.tile(u, j, side)[0], 2)
    pool.wait_ge(n.s_var, i + 2)
    nc.gpsimd.tensor_tensor(n.rstd[:, j % 2, :], n.var[:, j % 2, :], m.mhalf[:, :], ALU.pow).then_inc(n.s_rstd, 1)


def norm_shift(nc, dve, m, n, u, j):
    if n.sides(u, j):
        dve.wait_ge(n.s_rstd, u * 2 + j + 2)
        nc.vector.scalar_tensor_tensor(n.shift[:, j % 2, :], n.mv[:, j % 2, :, 0], -1.0, n.rstd[:, j % 2, :],
                                       ALU.mult, ALU.mult).then_inc(n.s_shift, 1)


def norm_apply(nc, act, n, u, j, side, x, readers):
    t, b = n.tile(u, j, side)
    act.wait_ge(n.s_shift, u * 2 + j + 2)
    for sem in readers:
        wait_reuse(act, sem, t, 2)
    nc.scalar.activation(n.out[side][:, b, :], x, ACT.Identity, bias=n.shift[:, j % 2, side:side + 1],
                         scale=n.rstd[:, j % 2, side:side + 1]).then_inc(n.s_out[side], 1)


def token_rows(m, t):
    return m.x[:, bass.ds(t, 1), :].rearrange("p o n -> p (o n)")


class Router:

    def __init__(self, nc, ctx, m, l, bank):
        e, k = l.experts, l.top
        name = f"route{l.n}"
        sb = lambda n, shape, dt=F32: ctx.enter_context(nc.sbuf_tensor(f"{name}_{n}", [P, 2] + shape, dt))
        sem = lambda n: m.phase.take(f"{name}_{n}")
        self.l, self.bank = l, bank
        self.logits_ps = bank[:, 256:256 + e]
        self.rank_ps = bank[:, 320:320 + e]
        self.count_ps = bank[:, 384:384 + e]
        self.hT = sb("hT", [DC, P])
        self.lg, self.top, self.negm = sb("logits", [e]), sb("top8", [8]), sb("neg_max", [1])
        self.idx = sb("index8", [8], U32)
        self.oh = sb("onehot", [k, e])
        self.sel = sb("chosen", [e], BF16)
        self.cum = ctx.enter_context(nc.sbuf_tensor(f"{name}_chosen_before", [P, e], BF16))
        self.place, self.prod = sb("place", [e]), sb("place_of_choice", [k, e])
        self.slot = sb("slot", [k], U32)
        self.cwk = sb("weight_of_choice", [2, 16])
        self.ex, self.sum, self.rs = sb("exps", [e]), sb("sum", [1]), sb("rsum", [1])
        self.ew, self.wt = sb("top_exps", [k]), sb("weights", [k])
        self.pay = sb("rows", [k, ROW])
        self.s_hT_ps, self.s_hT_sb, self.s_logits, self.s_lg, self.s_top, self.s_negm = sem("hT_ps"), sem("hT_sb"), sem("logits"), sem("lg"), sem("top"), sem("negm")
        self.s_idx, self.s_oh, self.s_sel, self.s_cum, self.s_rank, self.s_place = sem("idx"), sem("oh"), sem("sel"), sem("cum"), sem("rank"), sem("place")
        self.s_prod, self.s_slot, self.s_exps, self.s_w1, self.s_w2, self.s_w3 = sem("prod"), sem("slot"), sem("exps"), sem("w1"), sem("w2"), sem("w3")
        self.s_w4, self.s_weights, self.s_cwprod, self.s_cw, self.s_rows, self.s_dest = sem("w4"), sem("weights"), sem("cwprod"), sem("cw"), sem("rows"), sem("dest")
        self.s_sent = [sem("sent_even"), sem("sent_odd")]
        self.s_kept = [sem("hT_kept_even"), sem("hT_kept_odd")]
        self.s_counts, self.s_tab, self.s_rows_ps, self.s_tables = sem("counts"), sem("table_steps"), sem("table_rows_ps"), sem("tables")
        self.s_tail = sem("tails_zeroed")
        tb = lambda n, shape, dt=F32: ctx.enter_context(nc.sbuf_tensor(f"{name}_{n}", shape, dt))
        self.nf, self.ni, self.ti, self.tf = tb("n", [P, e]), tb("n_int", [P, e], I32), tb("tiles_int", [P, e], I32), tb("tiles", [P, e])
        self.ends, self.le, self.step, self.ls = tb("ends", [P, e]), tb("le", [P, e]), tb("step", [P, e]), tb("le_step", [P, e])
        self.onesf = tb("ones", [P, e])
        self.col = tb("col", [P, 4])


def router_pe_transpose(nc, pe, m, r, h, s_h, t, b):
    pe.wait_ge(s_h, t + 1)
    wait_reuse(pe, r.s_hT_sb, t, 1)
    wait_reuse(pe, r.s_lg, t, 1)
    wait_reuse(pe, r.s_place, t, 1)
    for c in range(DC):
        last = nc.tensor.transpose(r.bank[:, c * P:(c + 1) * P], h[:, b, c * P:(c + 1) * P], m.ident[:, :])
    last.then_inc(r.s_hT_ps, 1)


def router_act_hT(nc, act, m, r, t, b, u):
    act.wait_ge(r.s_hT_ps, t + 1)
    wait_reuse(act, r.s_logits, t, 2)
    if not isinstance(t, int) or t >= 2:
        act.wait_ge(r.s_kept[b], u * 16)
    nc.scalar.activation(r.hT[:, b, :, :], r.bank[:, 0:D].rearrange("p (c n) -> p c n", c=DC), ACT.Copy).then_inc(r.s_hT_sb, 1)


def router_sp_keep(nc, sp, m, r, t, b):
    sp.wait_ge(r.s_hT_sb, t + 1)
    sp.dma_start(m.hT[:, :, bass.ds(t * P, P)], r.hT[:, b, :, :]).then_inc(r.s_kept[b], 16)


def router_pe_logits(nc, pe, m, r, t, b):
    pe.wait_ge(r.s_hT_sb, t + 1)
    for c in range(DC):
        last = nc.tensor.matmul(r.logits_ps, r.hT[:, b, c, :], m.gate[r.l.n][:, c, :], start=(c == 0), stop=(c == DC - 1))
    last.then_inc(r.s_logits, 1)


def router_dve_choose(nc, dve, m, r, t, b):
    v, l = nc.vector, r.l
    e, k = l.experts, l.top
    dve.wait_ge(r.s_logits, t + 1)
    wait_reuse(dve, r.s_exps, t, 2)
    v.tensor_copy(r.lg[:, b, :], r.logits_ps).then_inc(r.s_lg, 1)
    dve.wait_ge(r.s_lg, t + 1)
    hold(dve, m)
    v.max(r.top[:, b, :], r.lg[:, b, :]).then_inc(r.s_top, 1)
    dve.wait_ge(r.s_top, t + 1)
    hold(dve, m)
    v.max_index(r.idx[:, b, :], r.top[:, b, :], r.lg[:, b, :]).then_inc(r.s_idx, 1)
    v.tensor_scalar(r.negm[:, b, :], r.top[:, b, 0:1], -1.0, None, ALU.mult).then_inc(r.s_negm, 1)
    dve.wait_ge(r.s_idx, t + 1)
    v.tensor_tensor(r.oh[:, b, :, :], m.iota_e[l.n][:, :, :], r.idx[:, b, 0:k].unsqueeze(2).to_broadcast([P, k, e]), ALU.is_equal).then_inc(r.s_oh, 1)
    dve.wait_ge(r.s_oh, t + 1)
    with nc.allow_low_precision("sums of ones"):
        v.tensor_reduce(r.sel[:, b, :], r.oh[:, b, :, :].rearrange("p k e -> p e k"), AX_X, ALU.add).then_inc(r.s_sel, 1)


def router_act_exps(nc, act, m, r, t, b):
    l = r.l
    act.wait_ge(r.s_negm, t + 1)
    wait_reuse(act, r.s_weights, t, 2)
    if l.n == 0:
        nc.scalar.activation(r.ex[:, b, :], r.lg[:, b, :], ACT.Exp, bias=r.negm[:, b, :], accum_out=r.sum[:, b, :])
        nc.scalar.activation(r.ew[:, b, :], r.top[:, b, 0:l.top], ACT.Exp, bias=r.negm[:, b, :]).then_inc(r.s_exps, 1)
    else:
        nc.scalar.activation(r.ew[:, b, :], r.top[:, b, 0:l.top], ACT.Exp, scale=-1.0).then_inc(r.s_exps, 1)


def router_pe_rank(nc, pe, m, r, t, b):
    pe.wait_ge(r.s_sel, t + 1)
    pe.wait_ge(r.s_cum, t + 1)
    nc.tensor.matmul(r.rank_ps, m.upper[:, :], r.sel[:, b, :], start=True, stop=False)
    nc.tensor.matmul(r.rank_ps, m.ones[:, :], r.cum[:, :], start=False, stop=True).then_inc(r.s_rank, 1)


def router_dve_place(nc, dve, m, r, t, b, u):
    v, l = nc.vector, r.l
    e, k = l.experts, l.top
    dve.wait_ge(r.s_rank, t + 1)
    v.tensor_tensor(r.place[:, b, :], r.rank_ps, m.list0[l.n][:, :], ALU.add).then_inc(r.s_place, 1)
    with nc.allow_low_precision("counts up to the number of tiles"):
        v.tensor_tensor(r.cum[:, :], r.cum[:, :], r.sel[:, b, :], ALU.add).then_inc(r.s_cum, 1)
    dve.wait_ge(r.s_place, t + 1)
    v.tensor_tensor(r.prod[:, b, :, :], r.oh[:, b, :, :], r.place[:, b, :].unsqueeze(1).to_broadcast([P, k, e]), ALU.mult).then_inc(r.s_prod, 1)
    dve.wait_ge(r.s_exps, t + 1)
    if l.n == 0:
        v.reciprocal(r.rs[:, b, :], r.sum[:, b, :]).then_inc(r.s_w1, 1)
    else:
        v.tensor_scalar(r.wt[:, b, :], r.ew[:, b, :], 1.0, None, ALU.add).then_inc(r.s_w1, 1)
    dve.wait_ge(r.s_prod, t + 1)
    if not isinstance(t, int) or t >= 2:
        dve.wait_ge(r.s_sent[b], u * (16 * k))
    with nc.allow_low_precision("whole numbers"):
        v.tensor_reduce(r.slot[:, b, :], r.prod[:, b, :, :], AX_X, ALU.add).then_inc(r.s_slot, 1)
    v.tensor_copy(r.pay[:, b, :, DEST:DEST + 1].bitcast(I32), m.dest[l.n][:, bass.ds(t, 1), :].rearrange("p o k -> p k o")).then_inc(r.s_dest, 1)
    dve.wait_ge(r.s_w1, t + 1)
    w_out = r.pay[:, b, :, WEIGHT:ROW].rearrange("p k o -> p (k o)")
    if l.n == 0:
        v.tensor_scalar(w_out, r.ew[:, b, :], r.rs[:, b, :], None, ALU.mult).then_inc(r.s_weights, 1)
        dve.wait_ge(r.s_weights, t + 1)
        for c in range(k):
            last = v.tensor_scalar(r.cwk[:, b, c, :], r.oh[:, b, c, :], r.pay[:, b, c, WEIGHT:ROW], None, ALU.mult)
        last.then_inc(r.s_cwprod, 1)
        dve.wait_ge(r.s_cwprod, t + 1)
        v.tensor_tensor(m.cw[:, bass.ds(t, 1), 0:e].rearrange("p o e -> p (o e)"), r.cwk[:, b, 0, :], r.cwk[:, b, 1, :], ALU.add).then_inc(r.s_cw, 1)
    else:
        v.reciprocal(r.wt[:, b, :], r.wt[:, b, :]).then_inc(r.s_w2, 1)
        dve.wait_ge(r.s_w2, t + 1)
        v.tensor_reduce(r.sum[:, b, :], r.wt[:, b, :], AX_X, ALU.add).then_inc(r.s_w3, 1)
        dve.wait_ge(r.s_w3, t + 1)
        v.tensor_scalar(r.sum[:, b, :], r.sum[:, b, :], 1e-20, None, ALU.add).then_inc(r.s_w4, 1)
        dve.wait_ge(r.s_w4, t + 1)
        v.reciprocal(r.rs[:, b, :], r.sum[:, b, :]).then_inc(r.s_cwprod, 1)
        dve.wait_ge(r.s_cwprod, t + 1)
        v.tensor_scalar(w_out, r.wt[:, b, :], r.rs[:, b, :], None, ALU.mult).then_inc(r.s_weights, 1)


def router_act_rows(nc, act, m, r, h, t, b, u):
    k = r.l.top
    if not isinstance(t, int) or t >= 2:
        act.wait_ge(r.s_sent[b], u * (16 * k))
    nc.scalar.activation(r.pay[:, b, :, 0:D], h[:, b, :].unsqueeze(1).to_broadcast([P, k, D]), ACT.Copy).then_inc(r.s_rows, 1)


def router_pool_send(nc, pool, m, r, t, b, choices):
    pool.wait_ge(r.s_rows, t + 1)
    pool.wait_ge(r.s_weights, t + 1)
    pool.wait_ge(r.s_slot, t + 1)
    pool.wait_ge(r.s_dest, t + 1)
    hold(pool, m)
    for k in choices:
        pool.indirect_dma_start(m.lists[r.l.n][:, :], bass.IndirectOffsetOnAxis(ap=r.slot[:, b, k:k + 1], axis=0),
                                r.pay[:, b, k, :], None).then_inc(r.s_sent[b], 16)


def router_pe_tables(nc, pe, m, r):
    pe.wait_ge(r.s_cum, NT + 1)
    pe.wait_ge(r.s_place, NT)
    nc.tensor.matmul(r.count_ps, m.ones[:, :], r.cum[:, :], start=True, stop=True).then_inc(r.s_counts, 1)
    pe.wait_ge(r.s_tab, 12)
    for n in range(2):
        last = nc.tensor.matmul(r.bank[0:1, n * P:(n + 1) * P], r.col[:, n:n + 1], m.ident[:, :], start=True, stop=True)
    last.then_inc(r.s_rows_ps, 1)


def router_dve_tables(nc, dve, m, r):
    v, l = nc.vector, r.l
    e = l.experts
    done = [0]

    def then(op):
        done[0] += 1
        op.then_inc(r.s_tab, 1)
        dve.wait_ge(r.s_tab, done[0])

    dve.wait_ge(r.s_counts, 1)
    then(v.memset(r.onesf[:, :], 1.0))
    then(v.tensor_copy(r.nf[:, :], r.count_ps))
    then(v.tensor_scalar(r.ni[:, :], r.nf[:, :], float(P - 1), None, ALU.add))
    then(v.tensor_scalar(r.ti[:, :], r.ni[:, :], P.bit_length() - 1, None, ALU.logical_shift_right))
    then(v.tensor_copy(r.tf[:, :], r.ti[:, :]))
    then(v.tensor_tensor_scan(r.ends[:, :], r.onesf[:, :], r.tf[:, :], 0.0, ALU.mult, ALU.add))
    then(v.tensor_scalar(r.le[:, :], r.ends[:, :], m.iota_p[:, :], None, ALU.is_le))
    then(v.tensor_scalar(r.step[:, :], r.tf[:, :], -float(P), float(LIST), ALU.mult, ALU.add))
    then(v.tensor_tensor(r.ls[:, :], r.le[:, :], r.step[:, :], ALU.mult))
    v.tensor_reduce(r.col[:, 2:3], r.le[:, :], AX_X, ALU.add)
    v.tensor_reduce(r.col[:, 3:4], r.ls[:, :], AX_X, ALU.add)
    then(v.tensor_tensor(m.tab[:, 2, 0:e], r.nf[0:1, :], m.list0[l.n][0:1, :], ALU.add))
    then(v.scalar_tensor_tensor(r.col[:, 1:2], m.iota_p[:, :], float(P), r.col[:, 3:4], ALU.mult, ALU.add))
    v.tensor_scalar(r.col[:, 0:1], r.col[:, 2:3], float(e - 1), None, ALU.min)
    then(v.tensor_scalar(r.col[:, 1:2], r.col[:, 1:2], float(l.zero_row), None, ALU.min))
    dve.wait_ge(r.s_rows_ps, 1)
    v.tensor_copy(m.tab[:, 0, TAB_PAD:TAB_PAD + P], r.bank[0:1, 0:P])
    v.tensor_copy(m.tab[:, 1, TAB_PAD:TAB_PAD + P], r.bank[0:1, P:2 * P]).then_inc(r.s_tables, 1)
    dve.wait_ge(r.s_tables, 1)


def router_sp_tails(nc, sp, m, r):
    l = r.l
    sp.wait_ge(r.s_tab, 10)
    with sp.Fori(0, l.experts) as e:
        row = sp.value_load(m.tab[0:1, 2, bass.ds(e, 1)], min_val=0, max_val=l.zero_row)
        sp.dma_start(m.lists[l.n][bass.ds(row, P), :], m.zrow[l.n][:, :]).then_inc(r.s_tail, 16)
    sp.wait_ge(r.s_tail, 16 * l.experts)


def tile_of(u, j, by, unroll=2):
    uu, jj = shifted(u, j, by, unroll)
    return uu * unroll + jj, jj, uu


def attend_heads(nc, m, a):
    l = LAYERS[0]
    ctx = ExitStack()
    with ctx:
        def sb(name, shape, dt=F32):
            return ctx.enter_context(nc.sbuf_tensor(name, shape, dt))

        def sem(name):
            return m.phase.take(name)

        q_ps, k_ps, v_ps, s_ps, pT_ps, o_ps, y_ps, h_ps = m.bank
        n = Norms(nc, ctx, m, "norm0", 2)
        r = Router(nc, ctx, m, l, h_ps)
        qT = sb("qT", [P, 2, DC, 2, S])
        kB = sb("kB", [P, 2, DC, 2, HC, S])
        vB = sb("vB", [P, 2, 2, HEADS // 2, 2 * HD + 2])
        sm, pr, pT = sb("scores", [P, 2, 512]), sb("probs", [P, 2, 512]), sb("probsT", [P, 2, 512])
        negmax, rec = sb("neg_row_max", [P, 2, HEADS]), sb("recip", [P, 2, HEADS])
        on, z = sb("attended", [P, 2, D]), sb("q_less_attended", [P, 2, D])

        ctxt = sb("context", [P, 2, D])
        s_init = sem("att_zeroed")
        s_ctx = [sem("context_even"), sem("context_odd")]
        s_qk, s_v = sem("qk_ps"), sem("v_ps")
        s_q_sb, s_k_sb, s_v_sb = sem("q_sb"), sem("k_sb"), sem("v_sb")
        s_sc, s_max, s_sub, s_exp = sem("scores_ps"), sem("row_max"), sem("scores_less_max"), sem("probs_done")
        s_pT, s_pT_sb, s_o, s_rec, s_on, s_z = sem("probsT_ps"), sem("probsT_sb"), sem("attended_ps"), sem("recip_done"), sem("attended_sb"), sem("z_done")
        s_y, s_x1 = sem("y_ps"), sem("x1_done")
        BH = P // HC

        with nc.Block() as block:

            @block.tensor
            def _(pe):
                mm = nc.tensor.matmul

                def project_qk(t, b, u):
                    pe.wait_ge(s_ctx[b], u * 16 + 16)
                    pe.wait_ge(n.s_out[Q], t + 1)
                    wait_reuse(pe, s_q_sb, t, 1)
                    wait_reuse(pe, s_k_sb, t, 1)
                    for c in range(DC):
                        mm(q_ps[:, c * P:(c + 1) * P], n.out[Q][:, b, c * P:(c + 1) * P], m.wq[:, :], start=True, stop=True)
                        last = mm(k_ps[:, c * P:(c + 1) * P], ctxt[:, b, c * P:(c + 1) * P], m.wk[:, :], start=True, stop=True)
                    last.then_inc(s_qk, 1)

                def project_v(t, b):
                    wait_reuse(pe, s_v_sb, t, 1)
                    for batch in range(2):
                        last = mm(v_ps[:, batch * D:(batch + 1) * D], m.wv[:, batch, :], ctxt[:, b, :], start=True, stop=True)
                    last.then_inc(s_v, 1)

                def scores(t, b):
                    pe.wait_ge(s_q_sb, t + 1)
                    pe.wait_ge(s_k_sb, t + 1)
                    wait_reuse(pe, s_sub, t, 1)
                    for batch in range(2):
                        for c in range(DC):
                            last = mm(s_ps[64 * batch:64 * batch + 64, c * 256:(c + 1) * 256], qT[:, b, c, batch, :],
                                      kB[:, b, c, batch, :, :], start=True, stop=True)
                    last.then_inc(s_sc, 1)

                def turn_probs(t, b):
                    pe.wait_ge(s_exp, t + 1)
                    wait_reuse(pe, s_pT_sb, t, 1)
                    for g in range(4):
                        last = nc.tensor.transpose(pT_ps[:, g * P:(g + 1) * P], pr[:, b, g * P:(g + 1) * P], m.ident[:, :])
                    last.then_inc(s_pT, 1)

                def attend(t, b):
                    pe.wait_ge(s_pT_sb, t + 1)
                    pe.wait_ge(s_v_sb, t + 1)
                    wait_reuse(pe, s_on, t, 1)
                    w = 2 * HD + 2
                    for batch in range(2):
                        for g in range(4):
                            last = mm(o_ps[64 * batch:64 * batch + 64, g * w:(g + 1) * w],
                                      pT[:, b, g * P + 64 * batch:g * P + 64 * batch + 64], vB[:, b, batch, g, :], start=True, stop=True)
                    last.then_inc(s_o, 1)

                def output(t, b):
                    pe.wait_ge(s_z, t + 1)
                    wait_reuse(pe, s_x1, t, 1)
                    mm(y_ps[:, 0:D], m.wo[:, :], z[:, b, :], start=True, stop=True).then_inc(s_y, 1)

                def step(u, j):
                    t, b, u0 = tile_of(u, j, 0)
                    t1, b1, _u = tile_of(u, j, -1)
                    t2, b2, _u = tile_of(u, j, -2)
                    t3, b3, _u = tile_of(u, j, -3)
                    if exists(t2, NT):
                        output(t2, b2)
                    if exists(t, NT):
                        project_qk(t, b, u0)
                    if exists(t1, NT):
                        turn_probs(t1, b1)
                    if exists(t3, NT):
                        router_pe_transpose(nc, pe, m, r, n.out[H], n.s_out[H], t3, b3)
                    if exists(t, NT):
                        project_v(t, b)
                    if exists(t3, NT):
                        router_pe_logits(nc, pe, m, r, t3, b3)
                    if exists(t1, NT):
                        attend(t1, b1)
                    if exists(t, NT):
                        scores(t, b)
                    if exists(t3, NT):
                        router_pe_rank(nc, pe, m, r, t3, b3)

                pe.wait_ge(s_init, 3)
                pipeline(pe, step, NT, 2, 0, 3)
                router_pe_tables(nc, pe, m, r)

            @block.scalar
            def _(act):
                copy = lambda o, i: nc.scalar.activation(o, i, ACT.Copy)

                def keep_qk(t, b):
                    act.wait_ge(s_qk, t + 1)
                    wait_reuse(act, s_sc, t, 2)
                    copy(qT[:, b, :, :, :], q_ps[:, 0:D].rearrange("p (c a s) -> p c a s", c=DC, a=2)).then_inc(s_q_sb, 1)
                    for h in range(HC):
                        rows = slice(BH * h, BH * h + BH)
                        last = copy(kB[rows, b, :, :, h, :], k_ps[rows, 0:D].rearrange("p (c a s) -> p c a s", c=DC, a=2))
                    last.then_inc(s_k_sb, 1)

                def keep_probsT(t, b):
                    act.wait_ge(s_pT, t + 1)
                    wait_reuse(act, s_o, t, 2)
                    copy(pT[:, b, :], pT_ps[:, :]).then_inc(s_pT_sb, 1)

                def exps(t, b):
                    act.wait_ge(s_sub, t + 1)
                    wait_reuse(act, s_pT, t, 2)
                    nc.scalar.activation(pr[:, b, :], sm[:, b, :], ACT.Exp, scale=float(HD) ** -0.5).then_inc(s_exp, 1)

                def step(u, j):
                    t, b, _u = tile_of(u, j, 0)
                    t1, b1, _u = tile_of(u, j, -1)
                    t3, b3, u3 = tile_of(u, j, -3)
                    if exists(t, NT):
                        keep_qk(t, b)
                    if exists(t1, NT):
                        keep_probsT(t1, b1)
                    if exists(t3, NT):
                        router_act_hT(nc, act, m, r, t3, b3, u3)
                    for side, readers in ((H, [r.s_hT_ps, r.s_rows]), (Q, [s_qk, s_z])):
                        if side in n.sides(u, j):
                            norm_apply(nc, act, n, u, j, side, token_rows(m, n.tile(u, j, side)[0]), readers)
                    if exists(t3, NT):
                        router_act_exps(nc, act, m, r, t3, b3)
                        router_act_rows(nc, act, m, r, n.out[H], t3, b3, u3)
                    if exists(t, NT):
                        exps(t, b)

                act.wait_ge(s_init, 3)
                pipeline(act, step, NT, 2, 1, 3)

            @block.gpsimd
            def _(pool):
                def subtract(t, b):
                    pool.wait_ge(s_on, t + 1)
                    wait_reuse(pool, s_y, t, 2)
                    nc.gpsimd.tensor_tensor(z[:, b, :], n.out[Q][:, b, :], on[:, b, :], ALU.subtract).then_inc(s_z, 1)

                def step(u, j):
                    t1, b1, _u = tile_of(u, j, -1)
                    t4, b4, _u = tile_of(u, j, -4)
                    if exists(t4, NT):
                        router_pool_send(nc, pool, m, r, t4, b4, range(l.top))
                    norm_rstd(nc, pool, m, n, u, j)
                    if exists(t1, NT):
                        subtract(t1, b1)

                pipeline(pool, step, NT, 2, 1, 4)
                for b in range(2):
                    pool.wait_ge(r.s_sent[b], 16 * l.top * NT // 2)

            @block.vector
            def _(dve):
                v = nc.vector

                def keep_v(t, b):
                    dve.wait_ge(s_v, t + 1)
                    wait_reuse(dve, s_o, t, 2)
                    for par in range(2):
                        rows = slice(64 * par, 64 * par + 64)
                        src = v_ps[rows, :].rearrange("p (a g h n) -> p a g h n", a=2, g=4, h=2)[:, :, :, par, :]
                        last = v.tensor_copy(vB[rows, b, :, :, HD * par:HD * par + HD], src)
                    last.then_inc(s_v_sb, 1)

                def scores_less_max(t, b):
                    dve.wait_ge(s_sc, t + 1)
                    heads = s_ps[:, :].rearrange("p (h e) -> p h e", h=HEADS)
                    v.tensor_reduce(negmax[:, b, :], heads, AX_X, ALU.max, negate=True).then_inc(s_max, 1)
                    dve.wait_ge(s_max, t + 1)
                    wait_reuse(dve, s_exp, t, 2)
                    v.tensor_tensor(sm[:, b, :].rearrange("p (h e) -> p h e", h=HEADS), heads,
                                    negmax[:, b, :].unsqueeze(2).to_broadcast([P, HEADS, S]), ALU.add).then_inc(s_sub, 1)

                def divide(t, b):
                    w = 2 * HD + 2
                    dve.wait_ge(s_o, t + 1)
                    o = o_ps[:, 0:4 * w].rearrange("p (g w) -> p g w", g=4)
                    v.reciprocal(rec[:, b, :].rearrange("p (g h) -> p g h", g=4), o[:, :, 2 * HD:w]).then_inc(s_rec, 1)
                    dve.wait_ge(s_rec, t + 1)
                    wait_reuse(dve, s_z, t, 2)
                    for par in range(2):
                        last = v.tensor_tensor(on[:, b, :].rearrange("p (g h n) -> p g h n", g=4, h=2)[:, :, par, :], o[:, :, HD * par:HD * par + HD],
                                               rec[:, b, :].rearrange("p (g h) -> p g h", g=4)[:, :, par:par + 1].to_broadcast([P, 4, HD]), ALU.mult)
                    last.then_inc(s_on, 1)

                def residual(t):
                    dve.wait_ge(s_y, t + 1)
                    v.tensor_tensor(token_rows(m, t), y_ps[:, 0:D], token_rows(m, t), ALU.add).then_inc(s_x1, 1)

                def step(u, j):
                    t0, b0, _u = tile_of(u, j, 1)
                    t, b, _u = tile_of(u, j, 0)
                    t1, b1, _u = tile_of(u, j, -1)
                    t2, b2, _u = tile_of(u, j, -2)
                    t3, b3, u3 = tile_of(u, j, -3)
                    if exists(t2, NT):
                        residual(t2)
                    if exists(t0, NT):
                        norm_stats(nc, dve, m, n, u, j, Q, token_rows(m, t0))
                    if exists(t2, NT):
                        dve.wait_ge(s_x1, t2 + 1)
                        norm_stats(nc, dve, m, n, u, j, H, token_rows(m, t2))
                    norm_var(nc, dve, m, n, u, j)
                    if exists(t, NT):
                        keep_v(t, b)
                    if exists(t3, NT):
                        router_dve_choose(nc, dve, m, r, t3, b3)
                    norm_shift(nc, dve, m, n, u, j)
                    if exists(t1, NT):
                        divide(t1, b1)
                    if exists(t, NT):
                        scores_less_max(t, b)
                    if exists(t3, NT):
                        router_dve_place(nc, dve, m, r, t3, b3, u3)

                v.memset(n.mv[:, :, :, :], 1.0)
                for op in (v.memset(kB[:, :, :, :, :, :], 0.0), v.memset(vB[:, :, :, :, :], 0.0)):
                    op.then_inc(s_init, 1)
                dve.wait_ge(s_init, 2)
                for par in range(2):
                    last = v.memset(vB[64 * par:64 * par + 64, :, :, :, 2 * HD + par:2 * HD + par + 1], 1.0)
                last.then_inc(s_init, 1)
                dve.wait_ge(s_init, 3)
                v.memset(r.cum[:, :], 0.0).then_inc(r.s_cum, 1)
                pipeline(dve, step, NT, 2, 1, 3)
                router_dve_tables(nc, dve, m, r)

            @block.sync
            def _(sp):
                def load(t, b):
                    wait_reuse(sp, s_v, t, 2)
                    sp.dma_start(ctxt[:, b, :], a["ctx"][bass.ds(t * P, P), :]).then_inc(s_ctx[b], 16)

                def step(u, j):
                    t, b, _u = tile_of(u, j, 1)
                    t3, b3, _u = tile_of(u, j, -3)
                    if exists(t, NT):
                        load(t, b)
                    if exists(t3, NT):
                        router_sp_keep(nc, sp, m, r, t3, b3)

                pipeline(sp, step, NT, 2, 1, 3)
                router_sp_tails(nc, sp, m, r)
                for b in range(2):
                    sp.wait_ge(r.s_kept[b], 16 * NT // 2)


class Shared:

    def __init__(self, nc, ctx, m, l):
        name = f"shared{l.n}"
        sem = lambda n: m.phase.take(f"{name}_{n}")
        self.l, self.chunks = l, len(l.shared)
        self.g_ps, self.u_ps, self.z_ps, self.cw_ps = m.bank[0:2], m.bank[2:4], m.bank[4:6], m.bank[6]
        self.act = ctx.enter_context(nc.sbuf_tensor(f"{name}_silu", [P, 2, 512], F32))
        self.hid = ctx.enter_context(nc.sbuf_tensor(f"{name}_hidden", [P, 2, self.chunks, 512], F32))
        self.s_gu, self.s_act, self.s_hid, self.s_z, self.s_x = sem("gate_up_ps"), sem("silu_done"), sem("hidden_done"), sem("out_ps"), sem("added")
        self.s_cw, self.s_cwT = sem("weights_ps"), sem("weights_sb")


BLOCK = 512
BLOCKS, BT = TOKENS // BLOCK, BLOCK // P


def shared_pe(nc, pe, m, s):
    mm, l = nc.tensor.matmul, s.l

    def down(blk):
        pe.wait_ge(s.s_hid, (blk + 1) * s.chunks)
        if l.bias:
            pe.wait_ge(s.s_cwT, blk + 1)
        for i in range(BT):
            t = blk * BT + i
            if t >= 2:
                pe.wait_ge(s.s_x, t - 1)
            z = s.z_ps[t % 2][:, 0:D]
            if l.bias:
                mm(z, m.cwT[:, t * P:(t + 1) * P], m.b2[:, :], start=True, stop=False)
            for c, (f0, fs) in enumerate(l.shared):
                last = mm(z, s.hid[0:fs, blk % 2, c, i * P:(i + 1) * P], m.sw_out[l.n][0:fs, c, :],
                          start=(c == 0 and not l.bias), stop=(c == s.chunks - 1))
            last.then_inc(s.s_z, 1)

    for blk in range(BLOCKS):
        cols = slice(blk * BLOCK, (blk + 1) * BLOCK)
        if l.bias:
            if blk:
                pe.wait_ge(s.s_cwT, blk)
            for i in range(BT):
                last = nc.tensor.transpose(s.cw_ps[0:17, i * P:(i + 1) * P], m.cw[:, blk * BT + i, :], m.ident[:, :])
            last.then_inc(s.s_cw, 1)
        for c, (f0, fs) in enumerate(l.shared):
            n = blk * s.chunks + c
            if n >= 2:
                pe.wait_ge(s.s_hid, n - 1)
            for half, bank in ((0, s.g_ps), (1, s.u_ps)):
                for d in range(DC):
                    last = mm(bank[n % 2][0:fs, :], m.sw_in[l.n][:, d, half * l.fs + f0:half * l.fs + f0 + fs], m.hT[:, d, cols],
                              start=(d == 0), stop=(d == DC - 1))
            last.then_inc(s.s_gu, 1)
        if blk:
            down(blk - 1)
    down(BLOCKS - 1)


def shared_act(nc, act, m, s):
    l = s.l
    for blk in range(BLOCKS):
        if l.bias:
            act.wait_ge(s.s_cw, blk + 1)
            nc.scalar.activation(m.cwT[:, blk * BLOCK:(blk + 1) * BLOCK], s.cw_ps[0:17, :], ACT.Copy).then_inc(s.s_cwT, 1)
        for c, (f0, fs) in enumerate(l.shared):
            n = blk * s.chunks + c
            act.wait_ge(s.s_gu, n + 1)
            if n >= 2:
                act.wait_ge(s.s_hid, n - 1)
            bias = m.sbias[0:fs, c, 0:1] if l.bias else 0.0
            nc.scalar.activation(s.act[0:fs, n % 2, :], s.g_ps[n % 2][0:fs, :], ACT.Silu, bias=bias).then_inc(s.s_act, 1)


def shared_dve(nc, dve, m, s):
    v, l = nc.vector, s.l

    def add(blk):
        for t in range(blk * BT, (blk + 1) * BT):
            dve.wait_ge(s.s_z, t + 1)
            v.tensor_tensor(m.x[:, t, :], s.z_ps[t % 2][:, 0:D], m.x[:, t, :], ALU.add).then_inc(s.s_x, 1)

    for blk in range(BLOCKS):
        for c, (f0, fs) in enumerate(l.shared):
            n = blk * s.chunks + c
            dve.wait_ge(s.s_act, n + 1)
            if blk >= 2:
                dve.wait_ge(s.s_z, (blk - 1) * BT)
            bias = m.sbias[0:fs, c, 1:2] if l.bias else 0.0
            v.scalar_tensor_tensor(s.hid[0:fs, blk % 2, c, :], s.u_ps[n % 2][0:fs, :], bias, s.act[0:fs, n % 2, :],
                                   ALU.add, ALU.mult).then_inc(s.s_hid, 1)
        if blk:
            add(blk - 1)
    add(BLOCKS - 1)


def shared_alone(nc, m, a, l):
    ctx = ExitStack()
    with ctx:
        m.cwT = ctx.enter_context(nc.sbuf_tensor("cwT", [17, TOKENS], F32))
        s = Shared(nc, ctx, m, l)
        with nc.Block() as block:

            @block.sync
            def _(sp):
                sp.dma_start(m.bias_in[:, :], a["b13"].rearrange("(o n) -> o n", o=1).to_broadcast([P, 16 * 352])).then_inc(m.sem_weights[0], 16)

            @block.tensor
            def _(pe):
                shared_pe(nc, pe, m, s)

            @block.scalar
            def _(act):
                shared_act(nc, act, m, s)

            @block.vector
            def _(dve):
                shared_dve(nc, dve, m, s)


def experts(nc, m, l):
    ctx = ExitStack()
    with ctx:
        def sb(name, shape, dt=F32):
            return ctx.enter_context(nc.sbuf_tensor(f"moe{l.n}_{name}", shape, dt))

        def sem(name):
            return m.phase.take(f"moe{l.n}_{name}")

        f, fc, kc, n = l.f, l.fchunk, l.f // l.fchunk, l.tiles
        xT_ps, gu_ps, hT_ps, y_ps = m.bank[0:2], m.bank[2:4], m.bank[4:6], m.bank[6:8]
        w_out = w_out_view(m, l)
        rows, y = sb("rows", [P, RING, ROW]), sb("y", [P, RING, D])
        xT, hT = sb("rowsT", [P, 2, DC, P]), sb("hiddenT", [fc, 2, kc, P])
        gu, sil, hid = sb("gate_up", [P, 2, 2 * f]), sb("silu", [P, 2, f]), sb("hidden", [P, 2, f])
        s_in, s_out = [sem(f"rows_in{i}") for i in range(RING)], [sem(f"rows_out{i}") for i in range(RING)]
        s_xT_ps, s_xT, s_gu_ps, s_gu = sem("rowsT_ps"), sem("rowsT_sb"), sem("gate_up_ps"), sem("gate_up_sb")
        s_sil, s_hid, s_hT_ps, s_hT, s_y_ps, s_y = sem("silu_done"), sem("hidden_done"), sem("hiddenT_ps"), sem("hiddenT_sb"), sem("y_ps"), sem("y_done")
        AHEAD = RING - 3

        with nc.Block() as block:

            @block.sync
            def _(sp):
                def load(u, j, row):
                    t, k, r = tile_of(u, j, 0, RING)
                    if not exists(t, n):
                        return
                    if not isinstance(t, int) or t >= RING:
                        sp.wait_ge(s_out[k], r * 16)
                    sp.dma_start(rows[:, k, :], m.lists[l.n][bass.ds(row[0], P), :]).then_inc(s_in[k], 16)

                sp.wait_ge(m.sem_zero_lists, 32)
                pipeline(sp, load, n, RING, 0, 0,
                         lambda i, count: table_values(nc, m, mybir.EngineType.SP, 1, i, count, l.zero_row))

            @block.tensor
            def _(pe):
                mm = nc.tensor.matmul

                def turn_rows(t, k, r):
                    pe.wait_ge(s_in[k], (r + 1) * 16)
                    wait_reuse(pe, s_xT, t, 2)
                    for c in range(DC):
                        last = nc.tensor.transpose(xT_ps[k % 2][:, c * P:(c + 1) * P], rows[:, k, c * P:(c + 1) * P], m.ident[:, :])
                    last.then_inc(s_xT_ps, 1)

                def gate_up(t, k, e):
                    pe.wait_ge(s_xT, t + 1)
                    wait_reuse(pe, s_hid, t, 2)
                    for c in range(DC):
                        last = mm(gu_ps[k % 2][:, 0:2 * f], xT[:, k % 2, c, :], m.w_in[:, c, bass.ds(e * (2 * f), 2 * f)], start=(c == 0), stop=(c == DC - 1))
                    last.then_inc(s_gu_ps, 1)

                def turn_hidden(t, k):
                    pe.wait_ge(s_hid, t + 1)
                    wait_reuse(pe, s_hT, t, 2)
                    for c in range(kc):
                        last = nc.tensor.transpose(hT_ps[k % 2][0:fc, c * P:(c + 1) * P], hid[:, k % 2, c * fc:(c + 1) * fc], m.ident[:, :])
                    last.then_inc(s_hT_ps, 1)

                def down(t, k, e):
                    pe.wait_ge(s_hT, t + 1)
                    wait_reuse(pe, s_y, t, 2)
                    for c in range(kc):
                        last = mm(y_ps[k % 2][:, 0:D], hT[:, k % 2, c, :], w_out[:, c, bass.ds(e * D, D)], start=(c == 0), stop=(c == kc - 1))
                    last.then_inc(s_y_ps, 1)

                def step(u, j, e):
                    t, k, r = tile_of(u, j, 0, RING)
                    p1, q1, _r = tile_of(u, j, -1, RING)
                    p2, q2, _r = tile_of(u, j, -2, RING)
                    p3, q3, _r = tile_of(u, j, -3, RING)
                    if exists(t, n):
                        turn_rows(t, k, r)
                    if exists(p1, n):
                        gate_up(p1, q1, e[2])
                    if exists(p2, n):
                        turn_hidden(p2, q2)
                    if exists(p3, n):
                        down(p3, q3, e[0])

                pe.wait_ge(m.sem_weights[l.n], (6 if l.bias else 5) * 16)
                pipeline(pe, step, n, RING, 0, 3,
                         lambda i, count: table_values(nc, m, mybir.EngineType.PE, 0, i - 3, count + 3, l.experts - 1))

            @block.scalar
            def _(act):
                def keep_rowsT(t, k):
                    act.wait_ge(s_xT_ps, t + 1)
                    wait_reuse(act, s_gu_ps, t, 2)
                    nc.scalar.activation(xT[:, k % 2, :, :], xT_ps[k % 2][:, 0:D].rearrange("p (c n) -> p c n", c=DC), ACT.Copy).then_inc(s_xT, 1)

                def silu(t, k):
                    if l.bias:
                        act.wait_ge(s_gu, t + 1)
                        src = gu[:, k % 2, 0:f]
                    else:
                        act.wait_ge(s_gu_ps, t + 1)
                        src = gu_ps[k % 2][:, 0:f]
                    wait_reuse(act, s_hid, t, 2)
                    nc.scalar.activation(sil[:, k % 2, :], src, ACT.Silu).then_inc(s_sil, 1)

                def scale(t, k, r):
                    act.wait_ge(s_y_ps, t + 1)
                    if not isinstance(t, int) or t >= RING:
                        act.wait_ge(s_out[k], r * 16)
                    nc.scalar.activation(y[:, k, :], y_ps[k % 2][:, 0:D], ACT.Copy, scale=rows[:, k, WEIGHT:ROW]).then_inc(s_y, 1)

                def step(u, j):
                    t, k, _r = tile_of(u, j, 0, RING)
                    p1, q1, _r = tile_of(u, j, -1, RING)
                    p3, q3, r3 = tile_of(u, j, -3, RING)
                    if exists(t, n):
                        keep_rowsT(t, k)
                    if exists(p1, n):
                        silu(p1, q1)
                    if exists(p3, n) and l.bias:
                        scale(p3, q3, r3)

                pipeline(act, step, n, RING, 0, 3)

            @block.vector
            def _(dve):
                v = nc.vector

                def add_bias(t, k, e):
                    dve.wait_ge(s_gu_ps, t + 1)
                    wait_reuse(dve, s_hid, t, 2)
                    v.tensor_tensor(gu[:, k % 2, :], gu_ps[k % 2][:, 0:2 * f], m.bias_in[:, bass.ds(e * (2 * f), 2 * f)], ALU.add).then_inc(s_gu, 1)

                def hidden(t, k):
                    dve.wait_ge(s_sil, t + 1)
                    wait_reuse(dve, s_hT_ps, t, 2)
                    up = gu[:, k % 2, f:2 * f] if l.bias else gu_ps[k % 2][:, f:2 * f]
                    v.tensor_tensor(hid[:, k % 2, :], up, sil[:, k % 2, :], ALU.mult).then_inc(s_hid, 1)

                def keep_hiddenT(t, k):
                    dve.wait_ge(s_hT_ps, t + 1)
                    wait_reuse(dve, s_y_ps, t, 2)
                    v.tensor_copy(hT[:, k % 2, :, :], hT_ps[k % 2][0:fc, 0:kc * P].rearrange("p (c n) -> p c n", c=kc)).then_inc(s_hT, 1)

                def scale(t, k, r):
                    dve.wait_ge(s_y_ps, t + 1)
                    if not isinstance(t, int) or t >= RING:
                        dve.wait_ge(s_out[k], r * 16)
                    v.tensor_scalar(y[:, k, :], y_ps[k % 2][:, 0:D], rows[:, k, WEIGHT:ROW], None, ALU.mult).then_inc(s_y, 1)

                def step(u, j, e=None):
                    p1, q1, _r = tile_of(u, j, -1, RING)
                    p2, q2, _r = tile_of(u, j, -2, RING)
                    p3, q3, r3 = tile_of(u, j, -3, RING)
                    if exists(p1, n) and l.bias:
                        add_bias(p1, q1, e[0])
                    if exists(p2, n):
                        keep_hiddenT(p2, q2)
                    if exists(p1, n):
                        hidden(p1, q1)
                    if exists(p3, n) and not l.bias:
                        scale(p3, q3, r3)

                if l.bias:
                    dve.wait_ge(m.sem_weights[l.n], 6 * 16)
                    pipeline(dve, step, n, RING, 0, 3,
                             lambda i, count: table_values(nc, m, mybir.EngineType.DVE, 0, i - 1, count, l.experts - 1))
                else:
                    pipeline(dve, step, n, RING, 0, 3)

            @block.gpsimd
            def _(pool):
                def send(u, j):
                    t, k, _r = tile_of(u, j, 0, RING)
                    if not exists(t, n):
                        return
                    pool.wait_ge(s_y, t + 1)
                    hold(pool, m)
                    pool.indirect_dma_start(m.res[l.n][:, :], bass.IndirectOffsetOnAxis(ap=rows[:, k, DEST:DEST + 1].bitcast(U32), axis=0),
                                            y[:, k, :], None, bounds_check=l.out_rows - 1, oob_is_err=False).then_inc(s_out[k], 16)

                pipeline(pool, send, n, RING, 0, 0)
                for k in range(RING):
                    pool.wait_ge(s_out[k], 16 * (n // RING))


def attend_masked(nc, m, a):
    l0, l = LAYERS
    ctx = ExitStack()
    with ctx:
        def sb(name, shape, dt=F32):
            return ctx.enter_context(nc.sbuf_tensor("masked_" + name, shape, dt))

        def sem(name):
            return m.phase.take("masked_" + name)

        qT_ps, kT_ps, s_ps, pT_ps, o_ps, h_ps = m.bank[0], m.bank[1], m.bank[2], m.bank[3], m.bank[4], m.bank[7]
        n = Norms(nc, ctx, m, "norm1", 1)
        r = Router(nc, ctx, m, l, h_ps)
        sh = Shared(nc, ctx, m, l)
        res = sb("results", [P, 2, l0.top * D])
        qT, kT, pT = sb("qT", [P, 2, D]), sb("kT", [P, 2, D]), sb("probsT", [P, 2, P])
        sm, pr = sb("scores", [P, 2, S]), sb("probs", [P, 2, P])
        negmax, sums, rec = sb("neg_row_max", [P, 2, 1]), sb("row_sum", [P, 2, 1]), sb("recip", [P, 2, 1])
        keep, fill, valid = sb("keep", [P, NT, S]), sb("fill", [P, NT, S]), sb("valid", [P, NT])
        ctxt, val = sb("context", [P, 2, D]), sb("values", [P, 2, D])
        s_ctx, s_val = [sem("context_even"), sem("context_odd")], [sem("values_even"), sem("values_odd")]
        s_init, s_mask = sem("zeroed"), sem("mask_steps")
        s_res = [sem("results_even"), sem("results_odd")]
        s_add, s_sum = sem("first_added"), sem("all_added")
        s_qT, s_qT_sb, s_kT_sb, s_sc, s_sm, s_filled, s_max, s_exp = (
            sem("qT_ps"), sem("qT_sb"), sem("kT_sb"), sem("scores_ps"), sem("scores_sb"), sem("scores_filled"), sem("row_max"), sem("probs_done"))
        s_rec, s_valid, s_pT, s_pT_sb, s_o, s_x = sem("recip_done"), sem("scale_done"), sem("probsT_ps"), sem("probsT_sb"), sem("out_ps"), sem("x_done")

        with nc.Block() as block:

            @block.sync
            def _(sp):
                def load_results(t, b):
                    wait_reuse(sp, s_sum, t, 2)
                    sp.dma_start(res[:, b, :], m.res[0][bass.ds(t * (P * l0.top), P * l0.top), :].rearrange("(p k) d -> p (k d)", k=l0.top)).then_inc(s_res[b], 16)

                def load_context(t, b):
                    wait_reuse(sp, s_qT, t, 2)
                    sp.dma_start(ctxt[:, b, :], a["ctx"][bass.ds(t * P, P), :]).then_inc(s_ctx[b], 16)

                def load_values(t, b):
                    wait_reuse(sp, s_o, t, 2)
                    sp.dma_start(val[:, b, :], a["ctx"][bass.ds(t * P, P), :]).then_inc(s_val[b], 16)

                def step(u, j):
                    t0, b0, _u = tile_of(u, j, 2)
                    t, b, _u = tile_of(u, j, 1)
                    t1, b1, _u = tile_of(u, j, 0)
                    t2, b2, _u = tile_of(u, j, -2)
                    if exists(t0, NT):
                        load_results(t0, b0)
                    if exists(t, NT):
                        load_context(t, b)
                    if exists(t1, NT):
                        load_values(t1, b1)
                    if exists(t2, NT):
                        router_sp_keep(nc, sp, m, r, t2, b2)

                pipeline(sp, step, NT, 2, 2, 2)
                router_sp_tails(nc, sp, m, r)
                for b in range(2):
                    sp.wait_ge(r.s_kept[b], 16 * NT // 2)

            @block.tensor
            def _(pe):
                mm = nc.tensor.matmul

                def turn(t, b, u):
                    pe.wait_ge(s_ctx[b], u * 16 + 16)
                    pe.wait_ge(n.s_out[Q], t + 1)
                    wait_reuse(pe, s_qT_sb, t, 1)
                    wait_reuse(pe, s_kT_sb, t, 1)
                    for c in range(DC):
                        nc.tensor.transpose(qT_ps[:, c * P:(c + 1) * P], n.out[Q][:, b, c * P:(c + 1) * P], m.ident[:, :])
                        last = nc.tensor.transpose(kT_ps[:, c * P:(c + 1) * P], ctxt[:, b, c * P:(c + 1) * P], m.ident[:, :])
                    last.then_inc(s_qT, 1)

                def scores(t, b):
                    pe.wait_ge(s_qT_sb, t + 1)
                    pe.wait_ge(s_kT_sb, t + 1)
                    wait_reuse(pe, s_sm, t, 1)
                    for batch in range(2):
                        rows = slice(64 * batch, 64 * batch + 64)
                        for c in range(DC):
                            cols = slice(c * P + 64 * batch, c * P + 64 * batch + 64)
                            last = mm(s_ps[rows, 0:S], qT[:, b, cols], kT[:, b, cols], start=(c == 0), stop=(c == DC - 1))
                    last.then_inc(s_sc, 1)

                def turn_probs(t, b):
                    pe.wait_ge(s_exp, t + 1)
                    wait_reuse(pe, s_pT_sb, t, 1)
                    nc.tensor.transpose(pT_ps[:, 0:P], pr[:, b, :], m.ident[:, :]).then_inc(s_pT, 1)

                def attend(t, b, u):
                    pe.wait_ge(s_val[b], u * 16 + 16)
                    pe.wait_ge(s_pT_sb, t + 1)
                    wait_reuse(pe, s_x, t, 1)
                    mm(o_ps[:, 0:D], pT[:, b, :], val[:, b, :], start=True, stop=True).then_inc(s_o, 1)

                def step(u, j):
                    t, b, u0 = tile_of(u, j, 0)
                    t1, b1, u1 = tile_of(u, j, -1)
                    t2, b2, _u = tile_of(u, j, -2)
                    if exists(t, NT):
                        turn(t, b, u0)
                    if exists(t1, NT):
                        turn_probs(t1, b1)
                    if exists(t2, NT):
                        router_pe_transpose(nc, pe, m, r, n.out[H], n.s_out[H], t2, b2)
                    if exists(t, NT):
                        scores(t, b)
                    if exists(t1, NT):
                        attend(t1, b1, u1)
                    if exists(t2, NT):
                        router_pe_logits(nc, pe, m, r, t2, b2)
                        router_pe_rank(nc, pe, m, r, t2, b2)

                pe.wait_ge(s_init, 1)
                pipeline(pe, step, NT, 2, 0, 2)
                pe.wait_ge(s_x, NT)
                router_pe_tables(nc, pe, m, r)
                for b in range(2):
                    pe.wait_ge(r.s_kept[b], 16 * NT // 2)
                shared_pe(nc, pe, m, sh)

            @block.scalar
            def _(act):
                copy = lambda o, i: nc.scalar.activation(o, i, ACT.Copy)

                def keep_qT(t, b):
                    act.wait_ge(s_qT, t + 1)
                    wait_reuse(act, s_sc, t, 2)
                    copy(qT[:, b, :], qT_ps[:, 0:D]).then_inc(s_qT_sb, 1)

                def exps(t, b):
                    act.wait_ge(s_max, t + 1)
                    wait_reuse(act, s_pT, t, 2)
                    wait_reuse(act, s_valid, t, 2)
                    for batch in range(2):
                        rows = slice(64 * batch, 64 * batch + 64)
                        last = nc.scalar.activation(pr[rows, b, 64 * batch:64 * batch + 64], sm[rows, b, :], ACT.Exp,
                                                    bias=negmax[rows, b, :], accum_out=sums[rows, b, :])
                    last.then_inc(s_exp, 1)

                def keep_pT(t, b):
                    act.wait_ge(s_pT, t + 1)
                    wait_reuse(act, s_o, t, 2)
                    copy(pT[:, b, :], pT_ps[:, 0:P]).then_inc(s_pT_sb, 1)

                def step(u, j):
                    t, b, _u = tile_of(u, j, 0)
                    t1, b1, _u = tile_of(u, j, -1)
                    t2, b2, u2 = tile_of(u, j, -2)
                    if exists(t, NT):
                        keep_qT(t, b)
                    if exists(t1, NT):
                        keep_pT(t1, b1)
                    if exists(t2, NT):
                        router_act_hT(nc, act, m, r, t2, b2, u2)
                    if exists(t, NT):
                        exps(t, b)
                    if exists(t2, NT):
                        router_act_exps(nc, act, m, r, t2, b2)
                    for side, readers in ((Q, [s_qT]), (H, [r.s_hT_ps, r.s_rows])):
                        if side in n.sides(u, j):
                            norm_apply(nc, act, n, u, j, side, token_rows(m, n.tile(u, j, side)[0]), readers)
                    if exists(t2, NT):
                        router_act_rows(nc, act, m, r, n.out[H], t2, b2, u2)

                load_experts(act, m, a, l)
                act.wait_ge(s_init, 1)
                pipeline(act, step, NT, 2, 1, 2)
                shared_act(nc, act, m, sh)

            @block.gpsimd
            def _(pool):
                def step(u, j):
                    t3, b3, _u = tile_of(u, j, -3)
                    half = l.top // 2
                    if exists(t3, NT):
                        router_pool_send(nc, pool, m, r, t3, b3, range(half))
                    norm_rstd(nc, pool, m, n, u, j)
                    if exists(t3, NT):
                        router_pool_send(nc, pool, m, r, t3, b3, range(half, l.top))

                pipeline(pool, step, NT, 2, 1, 3)
                for b in range(2):
                    pool.wait_ge(r.s_sent[b], 16 * l.top * NT // 2)

            @block.vector
            def _(dve):
                v = nc.vector

                def add_results(t, b, u):
                    dve.wait_ge(s_res[b], u * 16 + 16)
                    v.tensor_tensor(token_rows(m, t), token_rows(m, t), res[:, b, 0:D], ALU.add).then_inc(s_add, 1)
                    dve.wait_ge(s_add, t + 1)
                    v.tensor_tensor(token_rows(m, t), token_rows(m, t), res[:, b, D:2 * D], ALU.add).then_inc(s_sum, 1)

                def keep_kT(t, b):
                    dve.wait_ge(s_qT, t + 1)
                    wait_reuse(dve, s_sc, t, 2)
                    v.tensor_copy(kT[:, b, :], kT_ps[:, 0:D]).then_inc(s_kT_sb, 1)

                def mask_scores(t, b):
                    dve.wait_ge(s_sc, t + 1)
                    wait_reuse(dve, s_exp, t, 2)
                    v.scalar_tensor_tensor(sm[:, b, :], s_ps[:, 0:S], float(D) ** -0.5, keep[:, bass.ds(t, 1), :].rearrange("p o s -> p (o s)"),
                                           ALU.mult, ALU.mult).then_inc(s_sm, 1)
                    dve.wait_ge(s_sm, t + 1)
                    v.tensor_tensor(sm[:, b, :], sm[:, b, :], fill[:, bass.ds(t, 1), :].rearrange("p o s -> p (o s)"), ALU.add).then_inc(s_filled, 1)
                    dve.wait_ge(s_filled, t + 1)
                    v.tensor_reduce(negmax[:, b, :], sm[:, b, :], AX_X, ALU.max, negate=True).then_inc(s_max, 1)

                def residual(t, b):
                    dve.wait_ge(s_exp, t + 1)
                    v.reciprocal(rec[:, b, :], sums[:, b, :]).then_inc(s_rec, 1)
                    dve.wait_ge(s_rec, t + 1)
                    v.tensor_tensor(rec[:, b, :], rec[:, b, :], valid[:, bass.ds(t, 1)], ALU.mult).then_inc(s_valid, 1)
                    dve.wait_ge(s_valid, t + 1)
                    dve.wait_ge(s_o, t + 1)
                    v.scalar_tensor_tensor(token_rows(m, t), o_ps[:, 0:D], rec[:, b, :], token_rows(m, t), ALU.mult, ALU.add).then_inc(s_x, 1)

                def step(u, j):
                    t0, b0, u0 = tile_of(u, j, 1)
                    t, b, _u = tile_of(u, j, 0)
                    t1, b1, _u = tile_of(u, j, -1)
                    t2, b2, u2 = tile_of(u, j, -2)
                    if exists(t, NT):
                        keep_kT(t, b)
                    if exists(t0, NT):
                        add_results(t0, b0, u0)
                    if exists(t, NT):
                        mask_scores(t, b)
                    if exists(t1, NT):
                        residual(t1, b1)
                    if exists(t0, NT):
                        dve.wait_ge(s_sum, t0 + 1)
                        norm_stats(nc, dve, m, n, u, j, Q, token_rows(m, t0))
                    if exists(t1, NT):
                        dve.wait_ge(s_x, t1 + 1)
                        norm_stats(nc, dve, m, n, u, j, H, token_rows(m, t1))
                    norm_var(nc, dve, m, n, u, j)
                    if exists(t2, NT):
                        router_dve_choose(nc, dve, m, r, t2, b2)
                    norm_shift(nc, dve, m, n, u, j)
                    if exists(t2, NT):
                        router_dve_place(nc, dve, m, r, t2, b2, u2)

                v.memset(n.mv[:, :, :, :], 1.0)
                v.memset(pr[:, :, :], 0.0).then_inc(s_init, 1)
                v.tensor_scalar(keep[:, :, :], m.mask8[:, :, :], 1.0, None, ALU.mult).then_inc(s_mask, 1)
                dve.wait_ge(s_mask, 1)
                v.tensor_scalar(fill[:, :, :], keep[:, :, :], -1.0, 1e30, ALU.add, ALU.mult)
                v.tensor_reduce(valid[:, :], keep[:, :, :], AX_X, ALU.max).then_inc(s_mask, 1)
                dve.wait_ge(s_mask, 2)
                v.memset(r.cum[:, :], 0.0).then_inc(r.s_cum, 1)
                pipeline(dve, step, NT, 2, 1, 2)
                router_dve_tables(nc, dve, m, r)
                shared_dve(nc, dve, m, sh)


def finish(nc, m, out):
    l = LAYERS[1]
    ctx = ExitStack()
    with ctx:
        def sem(name):
            return m.phase.take("finish_" + name)

        res = ctx.enter_context(nc.sbuf_tensor("finish_results", [P, 2, l.top * D], F32))
        part = ctx.enter_context(nc.sbuf_tensor("finish_sums", [P, 2, 3 * D], F32))
        s_res = [sem("results_even"), sem("results_odd")]
        s_a, s_b, s_c, s_d = sem("six_to_three"), sem("three_to_two"), sem("two_to_one"), sem("summed")
        s_out = sem("stored")
        with nc.Block() as block:

            @block.sync
            def _(sp):
                def load(u, j):
                    t, b, _u = tile_of(u, j, 0)
                    if not exists(t, NT):
                        return
                    wait_reuse(sp, s_a, t, 2)
                    sp.dma_start(res[:, b, :], m.res[1][bass.ds(t * (P * l.top), P * l.top), :].rearrange("(p k) d -> p (k d)", k=l.top)).then_inc(s_res[b], 16)

                pipeline(sp, load, NT, 2, 0, 0)

            @block.vector
            def _(dve):
                v = nc.vector

                def step(u, j):
                    t, b, r = tile_of(u, j, 0)
                    if not exists(t, NT):
                        return
                    xt = m.x[:, bass.ds(t, 1), :].rearrange("p o n -> p (o n)")
                    dve.wait_ge(s_res[b], r * 16 + 16)
                    v.tensor_tensor(part[:, b, :], res[:, b, 0:3 * D], res[:, b, 3 * D:6 * D], ALU.add).then_inc(s_a, 1)
                    dve.wait_ge(s_a, t + 1)
                    v.tensor_tensor(xt, xt, part[:, b, 0:D], ALU.add).then_inc(s_b, 1)
                    v.tensor_tensor(part[:, b, D:2 * D], part[:, b, D:2 * D], part[:, b, 2 * D:3 * D], ALU.add).then_inc(s_c, 1)
                    dve.wait_ge(s_b, t + 1)
                    dve.wait_ge(s_c, t + 1)
                    v.tensor_tensor(xt, xt, part[:, b, D:2 * D], ALU.add).then_inc(s_d, 1)

                pipeline(dve, step, NT, 2, 0, 0)

            @block.scalar
            def _(act):
                with act.Fori(0, NT) as t:
                    act.wait_ge(s_d, t + 1)
                    act.dma_start(out.rearrange("(t p) d -> p t d", p=P)[:, bass.ds(t, 1), :], m.x[:, bass.ds(t, 1), :]).then_inc(s_out, 16)
                act.wait_ge(s_out, 16 * NT)


def kernel(**inputs):
    import numpy as np
    import concourse.bacc as bacc
    from concourse.bass_utils import run_bass_kernel_spmd as run

    i = {k: np.asarray(v) for k, v in inputs.items()}
    lay = np.ascontiguousarray
    arrays = {
        "x": lay(i["x"].reshape(TOKENS, D)),
        "ctx": lay(i["ctx_2048"].reshape(TOKENS, D)),
        "mask": lay(i["mask_BxS2_bk0"]),
        "wqT": lay(i["L0_xattn_W_q"].T), "wkT": lay(i["L0_xattn_W_k"].T),
        "wvT": lay(i["L0_xattn_W_v"].T), "woT": lay(i["L0_xattn_W_o"].T),
        "gate0": lay(i["L0_ffn_gate_w"].T),
        "w13": lay(np.concatenate([i["L0_ffn_w1"], i["L0_ffn_w3"]], 1).transpose(2, 0, 1).reshape(D, -1)),
        "b13": lay(np.concatenate([i["L0_ffn_b1"], i["L0_ffn_b3"]], 1).reshape(-1)),
        "w2": lay(i["L0_ffn_w2"].transpose(2, 0, 1).reshape(176, -1)),
        "b2aug": lay(np.concatenate([i["L0_ffn_b2"], i["L0_ffn_sb2"][None]], 0)),
        "sw13": lay(np.concatenate([i["L0_ffn_sw1"], i["L0_ffn_sw3"]], 0).T),
        "sb1": lay(i["L0_ffn_sb1"]), "sb3": lay(i["L0_ffn_sb3"]),
        "sw2": lay(i["L0_ffn_sw2"].T),
        "gate1": lay(i["L1_ffn_gate_w"]),
        "wgu": lay(np.concatenate([i["L1_ffn_wg"], i["L1_ffn_wu"]], 2).transpose(1, 0, 2).reshape(D, -1)),
        "wd": lay(i["L1_ffn_wd"].transpose(1, 0, 2).reshape(96, -1)),
        "sgu": lay(np.concatenate([i["L1_ffn_sg"], i["L1_ffn_su"]], 1)),
        "sd": lay(i["L1_ffn_sd"]),
    }
    nc = bacc.Bacc("TRN2", target_bir_lowering=False, num_devices=1)
    a = {k: nc.dram_tensor(f"in_{k}", v.shape, mybir.dt.from_np(v.dtype), kind="ExternalInput").ap()
         for k, v in arrays.items()}
    out = nc.dram_tensor("out_x", (TOKENS, D), F32, kind="ExternalOutput").ap()
    program(nc, a, out)
    r = run(nc, [{f"in_{k}": v for k, v in arrays.items()}], core_ids=[0])
    return r.results[0]["out_x"].reshape(B, S, D)
```
